# Optimizing a Trainium2 kernel written in Bass

```python
import numpy as np
import jax
import jax.numpy as jnp

def _softmax(x, axis=-1):
    return jax.nn.softmax(x, axis=axis)

def _gelu(x):
    return jax.nn.gelu(x, approximate=True)

def _silu(x):
    return jax.nn.silu(x)

def _sigmoid(x):
    return jax.nn.sigmoid(x)

def _layernorm(x, axis=-1, eps=1e-05):
    m = jnp.mean(x, axis=axis, keepdims=True)
    v = jnp.var(x, axis=axis, keepdims=True)
    return (x - m) / jnp.sqrt(v + eps)

def _scatter_add(tgt, idx, src, axis=0):
    return tgt.at[idx].add(src)

def _segment_sum(src, seg, n):
    return jax.ops.segment_sum(src, seg, n)
kernel_name = 'mk_gnn_resnorm_d2_gnn_r8_d7928c'

def setup_inputs(seed: int=0):
    np.random.seed(seed)
    _w = jnp.asarray

    def _rec_inputs():
        import jax
        import jax.numpy as jnp
        _gk = jax.random.key(seed)
        x = -0.0004287 + 1 * jax.random.normal(jax.random.fold_in(_gk, 1), (6250, 160), jnp.float32)
        src = jax.random.randint(jax.random.fold_in(_gk, 2), (200000,), 0, 6250, jnp.int32)
        dst = jnp.minimum((6250 * jax.random.uniform(jax.random.fold_in(_gk, 3), (200000,)) ** 2.0).astype(jnp.int32), 49999)
        _o = jnp.argsort(dst, stable=True)
        src = src[_o]
        dst = dst[_o]
        edge_attr_10 = jax.random.uniform(jax.random.fold_in(_gk, 12), (200000, 10), jnp.float32, 0.0, 1)
        edge_attr_4 = 0.000486536 + 0.999406 * jax.random.normal(jax.random.fold_in(_gk, 13), (200000, 4), jnp.float32)
        edge_attr_64 = 0.000127647 + 1.00004 * jax.random.normal(jax.random.fold_in(_gk, 14), (200000, 64), jnp.float32)
        node_vec1 = -0.00786984 + 0.999612 * jax.random.normal(jax.random.fold_in(_gk, 15), (6250, 1), jnp.float32)
        node_vec1_n2 = -0.00786984 + 0.999612 * jax.random.normal(jax.random.fold_in(_gk, 16), (6250, 1), jnp.float32)
        node_vec1_n3 = -0.00786984 + 0.999612 * jax.random.normal(jax.random.fold_in(_gk, 17), (6250, 1), jnp.float32)
        return (x, src, dst, edge_attr_10, edge_attr_4, edge_attr_64, node_vec1, node_vec1_n2, node_vec1_n3)
    x, src, dst, edge_attr_10, edge_attr_4, edge_attr_64, node_vec1, node_vec1_n2, node_vec1_n3 = _rec_inputs()

    def _L0_gnn_setup():
        import jax, jax.numpy as jnp
        import numpy as np
        N = 3125
        E = 50000
        S = 64
        V = 32
        NB = 10
        H = 100
        WN = 192
        MID = 96
        NUM_NEIGHBORS = 16.0
        C_S = float(np.sin(np.pi / 8.0))
        C_X = float(np.cos(np.pi / 8.0))
        SQRT3 = float(np.sqrt(3.0))

        def fctp_scalar_attr(xs, xv, attr, Ws, Wv):
            s = xs * attr @ Ws
            v = jnp.einsum('nuc,uo->noc', xv * attr[:, :, None], Wv)
            return (s, v)
        key = jax.random.key(seed)
        k = jax.random.split(key, 24)

        def w(i, shape):
            return jax.random.normal(k[i], shape, jnp.float32) / np.sqrt(float(shape[0]))
        return {'node_input': jax.random.normal(k[0], (N, S + 3 * V), jnp.float32), 'node_attr': jax.random.normal(k[1], (N, 1), jnp.float32), 'node_crystal_attr': jax.random.normal(k[2], (N, 1), jnp.float32), 'sym_mask': jax.random.normal(k[3], (N, 1), jnp.float32), 'edge_attr': jax.random.normal(k[4], (E, 4), jnp.float32), 'edge_length_embedded': jax.random.uniform(k[5], (E, NB), dtype=jnp.float32), 'edge_src': jax.random.randint(k[6], (E,), 0, N), 'edge_dst': jax.random.randint(k[7], (E,), 0, N), 'Ws_sc_a': w(8, (S, S)), 'Wv_sc_a': w(9, (V, V)), 'Ws_sc_c': w(10, (S, S)), 'Wv_sc_c': w(11, (V, V)), 'Ws_l1_a': w(12, (S, S)), 'Wv_l1_a': w(13, (V, V)), 'Ws_l1_c': w(14, (S, S)), 'Wv_l1_c': w(15, (V, V)), 'W_fc1': w(16, (NB, H)), 'W_fc2': w(17, (H, WN)), 'Ws_l2_a': w(18, (MID, MID)), 'Wv_l2_a': w(19, (MID, MID)), 'Ws_l2_c': w(20, (MID, MID)), 'Wv_l2_c': w(21, (MID, MID)), 'Ws_l3': w(22, (MID, S)), 'Wv_l3': w(23, (MID, V))}
    _L0_gnn_all = _L0_gnn_setup()
    _L0_gnn_in = {k: v for k, v in _L0_gnn_all.items() if k in ('Ws_sc_a', 'Wv_sc_a', 'Ws_sc_c', 'Wv_sc_c', 'Ws_l1_a', 'Wv_l1_a', 'Ws_l1_c', 'Wv_l1_c', 'W_fc1', 'W_fc2', 'Ws_l2_a', 'Wv_l2_a', 'Ws_l2_c', 'Wv_l2_c', 'Ws_l3', 'Wv_l3')}
    del _L0_gnn_all

    def _L1_gnn_setup():
        import jax, jax.numpy as jnp
        import numpy as np
        N, E = (5000, 80000)
        S_IN, V_IN = (64, 32)
        S_MID, V_MID = (96, 128)
        S_OUT, V_OUT = (96, 32)
        R = 64
        FC_HID = 64
        W_NUMEL = 64 + 64 + 32 + 32 + 32
        NUM_NEIGHBORS = 16.0

        def _inv(d):
            return 1.0 / jnp.sqrt(jnp.float32(d))

        def _forward(node_features, node_attr, edge_attr, edge_scalars, lin1_ws, lin1_wv, fc_w1, fc_w2, sc_ws, sc_wv, lin2_ws, lin2_wv, edge_src, edge_dst):
            n = node_features.shape[0]
            s = node_features[:, :S_IN]
            v = node_features[:, S_IN:].reshape(n, V_IN, 3)
            a = node_attr
            sc_s = s @ sc_ws * a * _inv(S_IN)
            sc_v = jnp.einsum('nci,cd->ndi', v, sc_wv) * a[:, :, None] * _inv(V_IN)
            h_s = s @ lin1_ws * a * _inv(S_IN)
            h_v = jnp.einsum('nci,cd->ndi', v, lin1_wv) * a[:, :, None] * _inv(V_IN)
            hid = jax.nn.silu(edge_scalars @ fc_w1 * _inv(R))
            w = hid @ fc_w2 * _inv(FC_HID)
            w1, w2, w3, w4, w5 = jnp.split(w, [64, 128, 160, 192], axis=-1)
            es = h_s[edge_src]
            ev = h_v[edge_src]
            e0 = edge_attr[:, :1]
            e1 = edge_attr[:, 1:4]
            m_s1 = w1 * es * e0
            m_s2 = w4 * jnp.einsum('eci,ei->ec', ev, e1) * _inv(3)
            m_v1 = (w2 * es)[:, :, None] * e1[:, None, :]
            m_v2 = w3[:, :, None] * ev * e0[:, :, None]
            m_v3 = w5[:, :, None] * jnp.cross(ev, e1[:, None, :]) * _inv(2)
            mid_s = jnp.concatenate([m_s1, m_s2], axis=-1)
            mid_v = jnp.concatenate([m_v1, m_v2, m_v3], axis=1)
            inv_nn = 1.0 / jnp.sqrt(jnp.float32(NUM_NEIGHBORS))
            agg_s = jax.ops.segment_sum(mid_s, edge_dst, num_segments=n) * inv_nn
            agg_v = jax.ops.segment_sum(mid_v, edge_dst, num_segments=n) * inv_nn
            o_s = agg_s @ lin2_ws * a * _inv(S_MID)
            o_v = jnp.einsum('nci,cd->ndi', agg_v, lin2_wv) * a[:, :, None] * _inv(V_MID)
            pre_s = sc_s + o_s
            pre_v = sc_v + o_v
            scalars = jax.nn.silu(pre_s[:, :64])
            gates = jax.nn.sigmoid(pre_s[:, 64:96])
            gated = gates[:, :, None] * pre_v
            return jnp.concatenate([scalars, gated.reshape(n, 3 * V_OUT)], axis=-1)
        key = jax.random.key(seed)
        ks = jax.random.split(key, 13)
        return {'node_features': jax.random.normal(ks[0], (N, S_IN + 3 * V_IN), jnp.float32), 'node_attr': jnp.ones((N, 1), jnp.float32), 'edge_src': jax.random.randint(ks[1], (E,), 0, N), 'edge_dst': jax.random.randint(ks[2], (E,), 0, N), 'edge_attr': jax.random.normal(ks[3], (E, 4), jnp.float32), 'edge_scalars': jax.random.normal(ks[4], (E, R), jnp.float32), 'lin1_ws': jax.random.normal(ks[5], (S_IN, S_IN), jnp.float32), 'lin1_wv': jax.random.normal(ks[6], (V_IN, V_IN), jnp.float32), 'fc_w1': jax.random.normal(ks[7], (R, FC_HID), jnp.float32), 'fc_w2': jax.random.normal(ks[8], (FC_HID, W_NUMEL), jnp.float32), 'sc_ws': jax.random.normal(ks[9], (S_IN, S_OUT), jnp.float32), 'sc_wv': jax.random.normal(ks[10], (V_IN, V_OUT), jnp.float32), 'lin2_ws': jax.random.normal(ks[11], (S_MID, S_OUT), jnp.float32), 'lin2_wv': jax.random.normal(ks[12], (V_MID, V_OUT), jnp.float32)}
    _L1_gnn_all = _L1_gnn_setup()
    _L1_gnn_in = {k: v for k, v in _L1_gnn_all.items() if k in ('lin1_ws', 'lin1_wv', 'fc_w1', 'fc_w2', 'sc_ws', 'sc_wv', 'lin2_ws', 'lin2_wv')}
    del _L1_gnn_all
    return {'x': x, 'src': src, 'dst': dst, 'edge_attr_10': edge_attr_10, 'edge_attr_4': edge_attr_4, 'edge_attr_64': edge_attr_64, 'node_vec1': node_vec1, 'node_vec1_n2': node_vec1_n2, 'node_vec1_n3': node_vec1_n3, 'L0_gnn_Ws_sc_a': _L0_gnn_in['Ws_sc_a'], 'L0_gnn_Wv_sc_a': _L0_gnn_in['Wv_sc_a'], 'L0_gnn_Ws_sc_c': _L0_gnn_in['Ws_sc_c'], 'L0_gnn_Wv_sc_c': _L0_gnn_in['Wv_sc_c'], 'L0_gnn_Ws_l1_a': _L0_gnn_in['Ws_l1_a'], 'L0_gnn_Wv_l1_a': _L0_gnn_in['Wv_l1_a'], 'L0_gnn_Ws_l1_c': _L0_gnn_in['Ws_l1_c'], 'L0_gnn_Wv_l1_c': _L0_gnn_in['Wv_l1_c'], 'L0_gnn_W_fc1': _L0_gnn_in['W_fc1'], 'L0_gnn_W_fc2': _L0_gnn_in['W_fc2'], 'L0_gnn_Ws_l2_a': _L0_gnn_in['Ws_l2_a'], 'L0_gnn_Wv_l2_a': _L0_gnn_in['Wv_l2_a'], 'L0_gnn_Ws_l2_c': _L0_gnn_in['Ws_l2_c'], 'L0_gnn_Wv_l2_c': _L0_gnn_in['Wv_l2_c'], 'L0_gnn_Ws_l3': _L0_gnn_in['Ws_l3'], 'L0_gnn_Wv_l3': _L0_gnn_in['Wv_l3'], 'L1_gnn_lin1_ws': _L1_gnn_in['lin1_ws'], 'L1_gnn_lin1_wv': _L1_gnn_in['lin1_wv'], 'L1_gnn_fc_w1': _L1_gnn_in['fc_w1'], 'L1_gnn_fc_w2': _L1_gnn_in['fc_w2'], 'L1_gnn_sc_ws': _L1_gnn_in['sc_ws'], 'L1_gnn_sc_wv': _L1_gnn_in['sc_wv'], 'L1_gnn_lin2_ws': _L1_gnn_in['lin2_ws'], 'L1_gnn_lin2_wv': _L1_gnn_in['lin2_wv']}

def reference(x, src, dst, edge_attr_10, edge_attr_4, edge_attr_64, node_vec1, node_vec1_n2, node_vec1_n3, L0_gnn_Ws_sc_a, L0_gnn_Wv_sc_a, L0_gnn_Ws_sc_c, L0_gnn_Wv_sc_c, L0_gnn_Ws_l1_a, L0_gnn_Wv_l1_a, L0_gnn_Ws_l1_c, L0_gnn_Wv_l1_c, L0_gnn_W_fc1, L0_gnn_W_fc2, L0_gnn_Ws_l2_a, L0_gnn_Wv_l2_a, L0_gnn_Ws_l2_c, L0_gnn_Wv_l2_c, L0_gnn_Ws_l3, L0_gnn_Wv_l3, L1_gnn_lin1_ws, L1_gnn_lin1_wv, L1_gnn_fc_w1, L1_gnn_fc_w2, L1_gnn_sc_ws, L1_gnn_sc_wv, L1_gnn_lin2_ws, L1_gnn_lin2_wv):
    import jax
    import jax.numpy as jnp

    def _L0_gnn_ref(node_input, node_attr, node_crystal_attr, sym_mask, edge_attr, edge_length_embedded, edge_src, edge_dst, Ws_sc_a, Wv_sc_a, Ws_sc_c, Wv_sc_c, Ws_l1_a, Wv_l1_a, Ws_l1_c, Wv_l1_c, W_fc1, W_fc2, Ws_l2_a, Wv_l2_a, Ws_l2_c, Wv_l2_c, Ws_l3, Wv_l3):
        import jax, jax.numpy as jnp
        import numpy as np
        N = 3125
        E = 50000
        S = 64
        V = 32
        NB = 10
        H = 100
        WN = 192
        MID = 96
        NUM_NEIGHBORS = 16.0
        C_S = float(np.sin(np.pi / 8.0))
        C_X = float(np.cos(np.pi / 8.0))
        SQRT3 = float(np.sqrt(3.0))

        def fctp_scalar_attr(xs, xv, attr, Ws, Wv):
            s = xs * attr @ Ws
            v = jnp.einsum('nuc,uo->noc', xv * attr[:, :, None], Wv)
            return (s, v)
        n = node_input.shape[0]
        xs = node_input[:, :S]
        xv = node_input[:, S:].reshape(n, V, 3)
        ssa, sva = fctp_scalar_attr(xs, xv, node_attr, Ws_sc_a, Wv_sc_a)
        ssc, svc = fctp_scalar_attr(xs, xv, node_crystal_attr, Ws_sc_c, Wv_sc_c)
        s_s, s_v = (ssa + ssc, sva + svc)
        l1a_s, l1a_v = fctp_scalar_attr(xs, xv, node_attr, Ws_l1_a, Wv_l1_a)
        l1c_s, l1c_v = fctp_scalar_attr(xs, xv, node_crystal_attr, Ws_l1_c, Wv_l1_c)
        x1s, x1v = (l1a_s + l1c_s, l1a_v + l1c_v)
        weight = jax.nn.silu(edge_length_embedded @ W_fc1) @ W_fc2
        w0 = weight[:, :S]
        w1 = weight[:, S:2 * S]
        w2 = weight[:, 2 * S:2 * S + V]
        w3 = weight[:, 2 * S + V:]
        gs = x1s[edge_src]
        gv = x1v[edge_src]
        e_s = edge_attr[:, :1]
        e_v = edge_attr[:, 1:]
        mid0a = w0 * gs * e_s
        mid0b = w3 * (jnp.einsum('euc,ec->eu', gv, e_v) / SQRT3)
        mid1a = w1[:, :, None] * gs[:, :, None] * e_v[:, None, :]
        mid1b = w2[:, :, None] * gv * e_s[:, :, None]
        edge_feat = jnp.concatenate([mid0a, mid0b, mid1a.reshape(-1, 3 * S), mid1b.reshape(-1, 3 * V)], axis=-1)
        agg = jax.ops.segment_sum(edge_feat, edge_dst, num_segments=n) / np.sqrt(NUM_NEIGHBORS)
        m_s = agg[:, :MID]
        m_v = agg[:, MID:].reshape(n, MID, 3)
        l2a_s, l2a_v = fctp_scalar_attr(m_s, m_v, node_attr, Ws_l2_a, Wv_l2_a)
        l2c_s, l2c_v = fctp_scalar_attr(m_s, m_v, node_crystal_attr, Ws_l2_c, Wv_l2_c)
        m_s, m_v = (l2a_s + l2c_s, l2a_v + l2c_v)
        o_s, o_v = fctp_scalar_attr(m_s, m_v, sym_mask, Ws_l3, Wv_l3)
        out_s = C_S * s_s + C_X * o_s
        out_v = C_S * s_v + C_X * o_v
        return jnp.concatenate([out_s, out_v.reshape(n, 3 * V)], axis=-1)

    def _L1_gnn_ref(node_features, node_attr, edge_src, edge_dst, edge_attr, edge_scalars, lin1_ws, lin1_wv, fc_w1, fc_w2, sc_ws, sc_wv, lin2_ws, lin2_wv):
        import jax, jax.numpy as jnp
        import numpy as np
        N, E = (5000, 80000)
        S_IN, V_IN = (64, 32)
        S_MID, V_MID = (96, 128)
        S_OUT, V_OUT = (96, 32)
        R = 64
        FC_HID = 64
        W_NUMEL = 64 + 64 + 32 + 32 + 32
        NUM_NEIGHBORS = 16.0

        def _inv(d):
            return 1.0 / jnp.sqrt(jnp.float32(d))

        def _forward(node_features, node_attr, edge_attr, edge_scalars, lin1_ws, lin1_wv, fc_w1, fc_w2, sc_ws, sc_wv, lin2_ws, lin2_wv, edge_src, edge_dst):
            n = node_features.shape[0]
            s = node_features[:, :S_IN]
            v = node_features[:, S_IN:].reshape(n, V_IN, 3)
            a = node_attr
            sc_s = s @ sc_ws * a * _inv(S_IN)
            sc_v = jnp.einsum('nci,cd->ndi', v, sc_wv) * a[:, :, None] * _inv(V_IN)
            h_s = s @ lin1_ws * a * _inv(S_IN)
            h_v = jnp.einsum('nci,cd->ndi', v, lin1_wv) * a[:, :, None] * _inv(V_IN)
            hid = jax.nn.silu(edge_scalars @ fc_w1 * _inv(R))
            w = hid @ fc_w2 * _inv(FC_HID)
            w1, w2, w3, w4, w5 = jnp.split(w, [64, 128, 160, 192], axis=-1)
            es = h_s[edge_src]
            ev = h_v[edge_src]
            e0 = edge_attr[:, :1]
            e1 = edge_attr[:, 1:4]
            m_s1 = w1 * es * e0
            m_s2 = w4 * jnp.einsum('eci,ei->ec', ev, e1) * _inv(3)
            m_v1 = (w2 * es)[:, :, None] * e1[:, None, :]
            m_v2 = w3[:, :, None] * ev * e0[:, :, None]
            m_v3 = w5[:, :, None] * jnp.cross(ev, e1[:, None, :]) * _inv(2)
            mid_s = jnp.concatenate([m_s1, m_s2], axis=-1)
            mid_v = jnp.concatenate([m_v1, m_v2, m_v3], axis=1)
            inv_nn = 1.0 / jnp.sqrt(jnp.float32(NUM_NEIGHBORS))
            agg_s = jax.ops.segment_sum(mid_s, edge_dst, num_segments=n) * inv_nn
            agg_v = jax.ops.segment_sum(mid_v, edge_dst, num_segments=n) * inv_nn
            o_s = agg_s @ lin2_ws * a * _inv(S_MID)
            o_v = jnp.einsum('nci,cd->ndi', agg_v, lin2_wv) * a[:, :, None] * _inv(V_MID)
            pre_s = sc_s + o_s
            pre_v = sc_v + o_v
            scalars = jax.nn.silu(pre_s[:, :64])
            gates = jax.nn.sigmoid(pre_s[:, 64:96])
            gated = gates[:, :, None] * pre_v
            return jnp.concatenate([scalars, gated.reshape(n, 3 * V_OUT)], axis=-1)
        return _forward(node_features, node_attr, edge_attr, edge_scalars, lin1_ws, lin1_wv, fc_w1, fc_w2, sc_ws, sc_wv, lin2_ws, lin2_wv, edge_src, edge_dst)
    x = _layernorm(x + _L0_gnn_ref(x, node_vec1, node_vec1_n2, node_vec1_n3, edge_attr_4, edge_attr_10, src, dst, L0_gnn_Ws_sc_a, L0_gnn_Wv_sc_a, L0_gnn_Ws_sc_c, L0_gnn_Wv_sc_c, L0_gnn_Ws_l1_a, L0_gnn_Wv_l1_a, L0_gnn_Ws_l1_c, L0_gnn_Wv_l1_c, L0_gnn_W_fc1, L0_gnn_W_fc2, L0_gnn_Ws_l2_a, L0_gnn_Wv_l2_a, L0_gnn_Ws_l2_c, L0_gnn_Wv_l2_c, L0_gnn_Ws_l3, L0_gnn_Wv_l3), axis=-1)
    x = _layernorm(x + _L1_gnn_ref(x, node_vec1, src, dst, edge_attr_4, edge_attr_64, L1_gnn_lin1_ws, L1_gnn_lin1_wv, L1_gnn_fc_w1, L1_gnn_fc_w2, L1_gnn_sc_ws, L1_gnn_sc_wv, L1_gnn_lin2_ws, L1_gnn_lin2_wv), axis=-1)
    return x

_drawn_inputs = setup_inputs


def setup_inputs(seed=0):
    import zlib

    import numpy as np

    out = dict(_drawn_inputs(seed))
    spreads = {}
    factors = {}
    for name, (base, spread) in spreads.items():
        noise = np.random.default_rng([zlib.crc32(name.encode()), seed]).standard_normal(out[name].shape)
        drawn = base * np.exp(spread * noise) if base else spread * noise
        out[name] = jnp.asarray(drawn.astype(out[name].dtype))
    for name, factor in factors.items():
        out[name] = (out[name] * factor).astype(out[name].dtype)
    return out
```

```python
from contextlib import ExitStack

import numpy as np
import concourse.bass as bass
from concourse import mybir

F32 = mybir.dt.float32
I32 = mybir.dt.int32
ALU = mybir.AluOpType
ACT = mybir.ActivationFunctionType

P = 128
NODES, EDGES = 6250, 200000
S, V = 64, 32
V3 = 3 * V
D = V3 + S
NB0, H0 = 10, 100
NB1, H1 = 64, 64
MID = 96
S1 = 96

TPU, UPB = 5, 2
NBODY = 5
NT = TPU * UPB * NBODY
NPAD = NT * P
assert NPAD > NODES and (TPU * UPB) % 2 == 0

TPG = 4
GE = TPG * P
GPB = 4
BODIES = -(-EDGES // (GE * GPB))
G = BODIES * GPB
EPAD = G * GE
T = G * TPG
WIN = 64
SUMW = NPAD + WIN
GQ = 4
GP = G // GQ
assert GP * GQ == G and GP <= P
TAB = 4
WPITCH = 256
MW = 512
WARM_UP = 10
GATHERED = 16 * TPG

C_S, C_X = float(np.sin(np.pi / 8)), float(np.cos(np.pi / 8))
INV_NN = 0.25
EPS = 1e-5
R3, R2 = 1 / float(np.sqrt(3)), 1 / float(np.sqrt(2))


class Layer:

    def __init__(self, index):
        self.index = index
        self.wn = 192 if index == 0 else 224
        self.row = 160 if index == 0 else 224
        self.chunks = 3 if index == 0 else 4
        self.tiles_per_product = 1 if index == 0 else 2
        self.kin = NB0 if index == 0 else 2 * NB1
        self.hid = H0 if index == 0 else 2 * H1
        self.group_cols = GE // self.tiles_per_product
        self.silu_scale = 1.0 if index == 0 else 1 / float(np.sqrt(NB1))
        self.act_comps = 2 if index == 0 else 3
        self.own = 3 if index == 0 else 5


def kept_tensors(nc, ctx):
    w = {}
    for name, shape, dt in (
        ("fc1_0", [NB0, H0], F32), ("fc2_0", [H0, 192], F32), ("fc1_1", [P, P], F32), ("fc2_1", [P, 480], F32),
        ("node_s0", [S, 256], F32), ("node_v0", [V3, 384], F32), ("node_s1", [S, 160], F32), ("node_v1", [V3, 192], F32),
        ("out0", [P, 640], F32), ("out1", [P, 480], F32), ("ident", [P, P], F32), ("iota", [P, WIN], F32),
        ("attr", [P, NT, 3], F32), ("masked", [P, NT, 2], F32), ("table", [1, G, TAB], I32),
    ):
        w[name] = ctx.enter_context(nc.sbuf_tensor("k_" + name, shape, dt))
    return w


def node_loop(engine, step):
    for j in range(TPU * UPB):
        step(j, j // TPU, 0, j // TPU, j % TPU)
    with engine.Fori(1, NBODY) as i:
        for j in range(TPU * UPB):
            step(TPU * UPB * i + j, UPB * i + j // TPU, i, j // TPU, j % TPU)


def unit_loop(engine, step):
    for s in range(UPB):
        step(s, 0, s)
    with engine.Fori(1, NBODY) as i:
        for s in range(UPB):
            step(UPB * i + s, i, s)


def at_least(engine, sem, value):
    if not (isinstance(value, int) and value <= 0):
        engine.wait_ge(sem, value)


def setup_phase(nc, d, w):
    with ExitStack() as ctx:
        def sb(name, shape, dt=F32):
            return ctx.enter_context(nc.sbuf_tensor(name, shape, dt))

        def sem(name):
            return ctx.enter_context(nc.semaphore(name))

        x_v = [sb(f"s_xv{i}", [V3, TPU * P]) for i in range(UPB)]
        x_s = [sb(f"s_xs{i}", [S, TPU * P]) for i in range(UPB)]
        l2 = sb("s_l2", [MID, 16, P])
        l3 = sb("s_l3", [MID, S + V])
        dst_by_group = sb("dst_by_group", [GP, GQ, GE], I32)
        dst_by_group_f = sb("dst_by_group_f", [GP, GQ, GE])
        lo_f, hi_f, span_f = sb("lo_f", [GP, GQ]), sb("hi_f", [GP, GQ]), sb("span_f", [GP, GQ])
        span_i, lo_i, extra_i = (sb(n, [GP, GQ], I32) for n in ("span_i", "lo_i", "extra_i"))
        lo_row, extra_row, before_row = (sb(n, [1, G], I32) for n in ("lo_row", "extra_row", "before_row"))
        scan = [sb(f"scan{i}", [1, G]) for i in range(2)]
        lo_all = sb("lo_all", [P, G], I32)
        lo_all_f = sb("lo_all_f", [P, G])
        dst_tile = sb("dst_tile_i", [P, T], I32)
        dst_rel = sb("dst_rel_new", [P, T])
        iota_i = sb("iota_i", [P, WIN], I32)
        part_a = [sb(f"part_a{i}", [P, D]) for i in range(2)]
        h0 = [sb(f"h0_{i}", [P, TPU, D]) for i in range(UPB)]
        ps_out = ctx.enter_context(nc.psum_tensor("ps_out", [P, 1024], F32))
        ps_node = [ctx.enter_context(nc.psum_tensor(f"s_psn{i}", [P, 512], F32)) for i in range(2)]

        weights_in, l_in, attr_in, dst_in, dtile_in = (sem(n) for n in ("weights_in", "l_in", "attr_in", "dst_in", "dtile_in"))
        pool_made = sem("pool_made")
        out0_done = sem("out0_done")
        scaled = sem("scaled")
        masked_done = sem("masked_done")
        grp = sem("grp")
        tab_out, tab_in, rel_out = sem("tab_out"), sem("tab_in"), sem("rel_out")
        x_in = [sem(f"s_x_in{i}") for i in range(UPB)]
        node_mm, part_ready, h_ready = sem("s_node_mm"), sem("s_part_ready"), sem("s_h_ready")
        h_out = [sem(f"s_h_out{i}") for i in range(UPB)]
        block = ctx.enter_context(nc.Block())

        SCALES = (
            ("node_s0", 128, 256, C_S), ("node_v0", 192, 384, C_S),
            ("fc2_0", 0, 160, INV_NN), ("fc2_0", 160, 192, INV_NN * R3),
            *(("fc2_1", c0 + WPITCH * k, c1 + WPITCH * k, factor) for k in range(2) for c0, c1, factor in (
                (0, 160, INV_NN / 8), (160, 192, INV_NN / 8 * R3), (192, 224, INV_NN / 8 * R2))),
            ("node_s1", 0, 160, 1 / 8), ("node_v1", 0, 192, 1 / float(np.sqrt(V))),
            ("out1", 0, 96, 1 / float(np.sqrt(128))), ("out1", 96, 192, 1 / float(np.sqrt(96))),
            ("out1", 192, 288, 1 / float(np.sqrt(128))), ("out1", 288, 384, 1 / float(np.sqrt(96))),
            ("out1", 384, 480, 1 / float(np.sqrt(128))),
        )
        DIRECT = ("node_v0", "node_s0", "fc1_0", "fc2_0", "fc1_1", "fc2_1", "node_s1", "node_v1", "out1")

        @block.sync
        def _(sp):
            for name in DIRECT:
                sp.dma_start(w[name][:, :], d[name]).then_inc(weights_in, 16)
            sp.dma_start(l2[:, :, :], d["l2"]).then_inc(l_in, 16)
            sp.dma_start(l3[:, :], d["l3"]).then_inc(l_in, 16)
            sp.wait_ge(grp, 6)
            sp.dma_start(d["lo_dram"].rearrange("(p q) -> p q", q=GQ), lo_i[:, :]).then_inc(tab_out, 16)
            sp.dma_start(d["extra_dram"].rearrange("(p q) -> p q", q=GQ), extra_i[:, :]).then_inc(tab_out, 16)
            sp.wait_ge(tab_out, 32)
            lo_line = d["lo_dram"].rearrange("(a g) -> a g", a=1)
            sp.dma_start(lo_all[:, :], lo_line.broadcast_to([P, G])).then_inc(tab_in, 16)
            sp.dma_start(lo_row[:, :], lo_line).then_inc(tab_in, 16)
            sp.dma_start(extra_row[:, :], d["extra_dram"].rearrange("(a g) -> a g", a=1)).then_inc(tab_in, 16)
            sp.wait_ge(grp, 9)
            sp.dma_start(d["dst_rel"], dst_rel[:, :]).then_inc(rel_out, 16)

            def store(unit, i, s):
                sp.wait_ge(h_ready, TPU * unit + TPU)
                rows = d["table0"][bass.ds(unit * (TPU * P), TPU * P), :].rearrange("(k p) n -> p k n", p=P)
                sp.dma_start(rows[:, :, 0:S], h0[s][:, :, V3:D]).then_inc(h_out[s], 16)
                sp.dma_start(rows[:, :, S:D], h0[s][:, :, 0:V3]).then_inc(h_out[s], 16)
            unit_loop(sp, store)
            for s in range(UPB):
                sp.wait_ge(h_out[s], 32 * NBODY)
            sp.wait_ge(rel_out, 16)

        @block.gpsimd
        def _(pool):
            nc.gpsimd.iota(iota_i[:, :], [[1, WIN]], base=0, channel_multiplier=0).then_inc(pool_made, 1)
            nc.gpsimd.memset(w["ident"][:, :], 0.0).then_inc(pool_made, 1)
            pool.wait_ge(pool_made, 2)
            nc.gpsimd.affine_select(out=w["ident"][:, :], in_=w["ident"][:, :], compare_op=ALU.not_equal, fill=1.0,
                                    base=0, pattern=[[-1, P]], channel_multiplier=1).then_inc(pool_made, 1)

            def load(unit, i, s):
                at_least(pool, node_mm, TPU * unit - TPU)
                cols = bass.ds(unit * (TPU * P), TPU * P)
                pool.dma_start(x_v[s][:, :], d["xT_v"][:, cols]).then_inc(x_in[s], 16)
                pool.dma_start(x_s[s][:, :], d["xT_s"][:, cols]).then_inc(x_in[s], 16)
            unit_loop(pool, load)

        @block.scalar
        def _(act):
            act.dma_start(w["attr"][:, :, :], d["attr"]).then_inc(attr_in, 16)
            act.dma_start(dst_by_group[:, :, :], d["dst_by_group"]).then_inc(dst_in, 16)
            act.dma_start(dst_tile[:, :], d["dst_tile"]).then_inc(dtile_in, 16)
            act.wait_ge(attr_in, 16)

            def part(n, unit, i, s, k):
                act.wait_ge(node_mm, n + 1)
                at_least(act, h_ready, n - 1)
                nc.scalar.activation(part_a[(TPU * s + k) % 2][:, :],
                                     ps_node[(TPU * s + k) % 2][:, 0:D], ACT.Copy,
                                     scale=w["attr"][:, bass.ds(n, 1), 0]).then_inc(part_ready, 1)
            node_loop(act, part)

        @block.tensor
        def _(pe):
            pe.wait_ge(l_in, 32)
            for c in range(16):
                vec = c not in (6, 7, 14, 15)
                col = OUT0_COLUMNS[c] + (64 if c >= 12 else 0)
                n = V if vec else S
                last = nc.tensor.matmul(ps_out[:, col:col + n], l2[:, c, :], l3[:, S:S + V] if vec else l3[:, 0:S],
                                        start=True, stop=True)
            last.then_inc(out0_done, 1)
            pe.wait_ge(weights_in, 16 * len(DIRECT))

            def project(n, unit, i, s, k):
                if k == 0:
                    pe.wait_ge(x_in[s], 32 * i + 32)
                at_least(pe, h_ready, n - 1)
                out = ps_node[(TPU * s + k) % 2][:, 0:2 * D].rearrange("p (a n) -> p a n", a=2)
                nc.tensor.matmul(out[:, :, 0:V3], x_v[s][:, k * P:(k + 1) * P], w["node_v0"][:, 0:192], start=True, stop=True)
                nc.tensor.matmul(out[:, :, V3:D], x_s[s][:, k * P:(k + 1) * P], w["node_s0"][:, 0:128],
                                 start=True, stop=True).then_inc(node_mm, 1)
            node_loop(pe, project)

        @block.vector
        def _(dve):
            dve.wait_ge(dst_in, 16)
            nc.vector.tensor_scalar(dst_by_group_f[:, :, :], dst_by_group[:, :, :], float(NPAD - 1), None, ALU.min).then_inc(grp, 1)
            dve.wait_ge(grp, 1)
            nc.vector.tensor_reduce(lo_f[:, :], dst_by_group_f[:, :, :], mybir.AxisListType.X, ALU.min)
            nc.vector.tensor_reduce(hi_f[:, :], dst_by_group_f[:, :, :], mybir.AxisListType.X, ALU.max).then_inc(grp, 1)
            dve.wait_ge(grp, 2)
            nc.vector.tensor_copy(lo_i[:, :], lo_f[:, :]).then_inc(grp, 1)
            nc.vector.tensor_tensor(span_f[:, :], hi_f[:, :], lo_f[:, :], ALU.subtract).then_inc(grp, 1)
            dve.wait_ge(grp, 4)
            nc.vector.tensor_copy(span_i[:, :], span_f[:, :]).then_inc(grp, 1)
            dve.wait_ge(grp, 5)
            nc.vector.tensor_scalar(extra_i[:, :], span_i[:, :], WIN.bit_length() - 1, None, ALU.arith_shift_right).then_inc(grp, 1)

            dve.wait_ge(weights_in, 16 * len(DIRECT))
            for name, c0, c1, factor in SCALES[:2]:
                nc.vector.tensor_scalar(w[name][:, c0:c1], w[name][:, c0:c1], factor, None, ALU.mult)
            dve.wait_ge(attr_in, 16)

            def add_c(n, unit, i, s, k):
                dve.wait_ge(part_ready, n + 1)
                if k == 0:
                    at_least(dve, h_out[s], 32 * i)
                nc.vector.scalar_tensor_tensor(
                    out=h0[s][:, k, :], in0=ps_node[(TPU * s + k) % 2][:, D:2 * D], scalar=w["attr"][:, bass.ds(n, 1), 1],
                    in1=part_a[(TPU * s + k) % 2][:, :], op0=ALU.mult, op1=ALU.add).then_inc(h_ready, 1)

            dve.wait_ge(tab_in, 48)
            dve.wait_ge(dtile_in, 16)
            nc.vector.tensor_copy(lo_all_f[:, :], lo_all[:, :])
            nc.vector.tensor_scalar(dst_rel[:, :], dst_tile[:, :], float(NPAD - 1), None, ALU.min).then_inc(grp, 1)
            dve.wait_ge(grp, 7)
            rel = dst_rel[:, :].rearrange("p (g t) -> p g t", t=TPG)
            nc.vector.tensor_tensor(rel, rel, lo_all_f[:, :].unsqueeze(2).broadcast_to([P, G, TPG]), ALU.subtract).then_inc(grp, 1)
            nc.vector.tensor_copy(scan[0][:, :], extra_row[:, :]).then_inc(grp, 1)
            node_loop(dve, add_c)

            count = 9
            shift, n = 1, 0
            while shift < G:
                a, b = scan[n % 2], scan[(n + 1) % 2]
                dve.wait_ge(grp, count)
                nc.vector.tensor_copy(b[:, 0:shift], a[:, 0:shift])
                nc.vector.tensor_tensor(b[:, shift:G], a[:, shift:G], a[:, 0:G - shift], ALU.add).then_inc(grp, 1)
                shift, n, count = 2 * shift, n + 1, count + 1
            dve.wait_ge(grp, count)
            nc.vector.tensor_tensor(before_row[:, :], scan[n % 2][:, :], extra_row[:, :], ALU.subtract).then_inc(grp, 1)
            dve.wait_ge(grp, count + 1)
            for c, row in enumerate((lo_row, extra_row, before_row)):
                nc.vector.tensor_copy(w["table"][:, :, c], row[:, :])
            nc.vector.memset(w["table"][:, :, 3], 0)

            for name, c0, c1, factor in SCALES[2:]:
                nc.vector.tensor_scalar(w[name][:, c0:c1], w[name][:, c0:c1], factor, None, ALU.mult)
            dve.wait_ge(out0_done, 1)
            nc.vector.tensor_scalar(w["out0"][:, 0:448], ps_out[:, 0:448], C_X, None, ALU.mult)
            nc.vector.tensor_scalar(w["out0"][:, 448:640], ps_out[:, 512:704], C_X, None, ALU.mult)
            for c in range(2):
                nc.vector.tensor_tensor(w["masked"][:, :, c], w["attr"][:, :, c], w["attr"][:, :, 2], ALU.mult)
            dve.wait_ge(pool_made, 3)
            nc.vector.tensor_copy(w["iota"][:, :], iota_i[:, :]).then_inc(scaled, 1)
            dve.wait_ge(scaled, 1)


OUT0_COLUMNS = [0, 32, 64, 160, 192, 224, 96, 256, 320, 352, 384, 416, 448, 544, 480, 576]


def edge_phase(nc, d, w, sums, layer):
    L = layer.index
    table_dram = d[f"table{L}"]
    with ExitStack() as ctx:
        def sb(name, shape, dt=F32):
            return ctx.enter_context(nc.sbuf_tensor(f"e{L}_{name}", shape, dt))

        def psum(name, shape):
            return ctx.enter_context(nc.psum_tensor(f"e{L}_{name}", shape, F32))

        def sem(name):
            return ctx.enter_context(nc.semaphore(f"e{L}_{name}"))

        index = [sb(f"index{q}", [P, 2 * TPG], I32) for q in range(2)]
        attr = [sb(f"attr{q}", [P, 2 * TPG, 6]) for q in range(2)]
        inputs = [sb(f"inputs{q}", [layer.kin, 2 * layer.group_cols]) for q in range(2)]
        rows = [sb(f"rows{j}", [P, TPG, layer.row]) for j in range(GPB)]
        msg = [sb(f"msg{j}", [P, TPG, MW]) for j in range(GPB)]
        hidden = [sb(f"hidden{b}", [layer.hid, layer.group_cols]) for b in range(2)]
        dots = sb("dots", [P, TPG, 3, V])
        cross_b = sb("cross_b", [P, TPG, V3])
        match = [sb(f"match{b}", [P, TPG, WIN]) for b in range(2)]
        match_x = sb("match_x", [P, TPG, WIN])
        dst_rel = sb("dst_rel", [P, T])

        ps_w = [psum(f"w{b}", [P, TPG * WPITCH]) for b in range(2)]
        ps_h = psum("h", [P, GE])
        ps_sum = [psum(f"sum{b}", [P, 2, 4, WIN]) for b in range(2)]
        ps_misc = psum("misc", [P, 512])
        iota = ps_misc[:, 0:WIN]
        e_p = ps_misc[:, 64:112].rearrange("p (t c) -> p t c", c=6)
        cross_a = ps_misc[:, 112:496].rearrange("p (t n) -> p t n", t=TPG)

        prepared, dst_in = sem("prepared"), sem("dst_in")
        index_in = [sem(f"index_in{q}") for q in range(2)]
        attr_in = [sem(f"attr_in{q}") for q in range(2)]
        inputs_in = [sem(f"inputs_in{q}") for q in range(2)]
        gathered = [sem(f"gathered{j}") for j in range(GPB)]
        rows_free = [sem(f"rows_free{j}") for j in range(GPB)]
        hid_done, silu_done, w_done = sem("hid_done"), sem("silu_done"), sem("w_done")
        e_copied, own, act_parts = sem("e_copied"), sem("own"), sem("act_parts")
        matched, msg_done = sem("matched"), sem("msg_done")
        sum_done, added = sem("sum_done"), sem("added")
        x_rel, x_matched, x_sum_done, x_added = sem("x_rel"), sem("x_matched"), sem("x_sum_done"), sem("x_added")
        block = ctx.enter_context(nc.Block())

        def group_loop(engine, step):
            for j in range(GPB):
                step(0, j)
            with engine.Fori(1, BODIES) as i:
                for j in range(GPB):
                    step(i, j)

        @block.sync
        def _(sp):
            sp.dma_start(dst_rel[:, :], d["dst_rel"]).then_inc(dst_in, 16)

            def load(i, q):
                tiles = bass.ds((2 * i + q) * (2 * TPG), 2 * TPG)
                if not isinstance(i, int):
                    for j in (2 * q, 2 * q + 1):
                        sp.wait_ge(gathered[j], GATHERED * i)
                sp.dma_start(index[q][:, :], d["src"][:, tiles]).then_inc(index_in[q], 16)
                if not isinstance(i, int):
                    sp.wait_ge(hid_done, GPB * i - GPB + 2 * q + 2)
                cols = 2 * layer.group_cols
                sp.dma_start(inputs[q][:, :], d[f"inputs{L}"][:, bass.ds((2 * i + q) * cols, cols)]).then_inc(inputs_in[q], 16)
                if not isinstance(i, int):
                    sp.wait_ge(msg_done, GPB * i - GPB + 2 * q + 2)
                sp.dma_start(attr[q][:, :, :], d["edge_attr"][:, tiles, :]).then_inc(attr_in[q], 16)
            for q in range(2):
                load(0, q)
            with sp.Fori(1, BODIES) as i:
                for q in range(2):
                    load(i, q)

        @block.gpsimd
        def _(pool):
            for c in (2, 3):
                nc.gpsimd.memset(sums[:, c, :], 0.0).then_inc(prepared, 1)

            def gather(count, j):
                q = j // 2
                pool.wait_ge(prepared, 2)
                pool.wait_ge(index_in[q], count)
                pool.wait_ge(rows_free[j], count)
                for t in range(TPG):
                    c = (j % 2) * TPG + t
                    pool.indirect_dma_start(
                        out=rows[j][:, t, :], out_offset=None, in_=table_dram,
                        in_offset=bass.IndirectOffsetOnAxis(ap=index[q][:, c:c + 1], axis=0),
                    ).then_inc(gathered[j], 16)
            for j in range(GPB):
                gather(16, j)
            with pool.Fori(32, 16 * BODIES + 16, 16) as count:
                for j in range(GPB):
                    gather(count, j)

        @block.scalar
        def _(act):
            def parts(i, j):
                g, q, e0 = GPB * i + j, j // 2, (j % 2) * TPG
                act.wait_ge(hid_done, g + 1)
                at_least(act, w_done, g - 1)
                nc.scalar.activation(hidden[j % 2][:, :], ps_h[0:layer.hid, 0:layer.group_cols], ACT.Silu,
                                     scale=layer.silu_scale).then_inc(silu_done, 1)
                act.wait_ge(gathered[j], GATHERED * i + GATHERED)
                if j % 2 == 0:
                    act.wait_ge(attr_in[q], 16 * i + 16)
                at_least(act, matched, g - 1)
                for t in range(TPG):
                    e, m, r = attr[q][:, e0 + t, :], msg[j][:, t, :], rows[j][:, t, :]
                    last = nc.scalar.activation(m[:, 192:352], r[:, 0:160], ACT.Copy, scale=e[:, 0:1])
                    for c in range(layer.act_comps):
                        last = nc.scalar.activation(m[:, 64 * c:64 * c + 64], r[:, 0:64], ACT.Copy, scale=e[:, c + 1:c + 2])
                last.then_inc(act_parts, 1)
            group_loop(act, parts)

        @block.tensor
        def _(pe):
            def hid(i, j):
                if j % 2 == 0:
                    pe.wait_ge(inputs_in[j // 2], 16 * i + 16)
                at_least(pe, silu_done, GPB * i + j)
                n = layer.group_cols
                nc.tensor.matmul(ps_h[0:layer.hid, 0:n], w[f"fc1_{L}"][:, :], inputs[j // 2][:, (j % 2) * n:(j % 2) * n + n],
                                 start=True, stop=True).then_inc(hid_done, 1)

            def edge_weights(i, o):
                j = o % GPB
                pe.wait_ge(silu_done, GPB * i + o + 1)
                at_least(pe, msg_done, GPB * i + o - 1)
                for u in range(TPG // layer.tiles_per_product):
                    c0, n = u * layer.tiles_per_product * WPITCH, w[f"fc2_{L}"].shape[1]
                    last = nc.tensor.matmul(ps_w[j % 2][:, c0:c0 + n], hidden[j % 2][:, u * P:(u + 1) * P], w[f"fc2_{L}"][:, :],
                                            start=True, stop=True)
                last.then_inc(w_done, 1)

            def window_sums(j, matches):
                for c in range(layer.chunks):
                    for t in range(TPG):
                        for half in (0, P // 2):
                            f = c * P + half
                            last = nc.tensor.matmul(ps_sum[j % 2][half:half + P // 2, 0, c, :], msg[j][:, t, f:f + P // 2],
                                                    matches[:, t, :], start=(t == 0), stop=(t == TPG - 1))
                return last

            def sum_group(i, o):
                g, j = GPB * i + o, o % GPB
                extras = pe.value_load(w["table"][0:1, bass.ds(g, 1), 1:2], min_val=0, max_val=NPAD // WIN - 1)
                pe.wait_ge(msg_done, g + 1)
                window_sums(j, match[j % 2]).then_inc(sum_done, 1)
                with pe.If(extras):
                    before = pe.value_load(w["table"][0:1, bass.ds(g, 1), 2:3], min_val=0, max_val=G * (NPAD // WIN))
                    with pe.Fori(0, extras) as x:
                        pe.wait_ge(x_matched, before + x + 1)
                        window_sums(j, match_x).then_inc(x_sum_done, 1)

            for j in range(GPB):
                hid(0, j)
                if j >= 1:
                    edge_weights(0, j - 1)
                if j >= 2:
                    sum_group(0, j - 2)
            pe.wait_ge(silu_done, GPB)
            for c in range(WARM_UP):
                nc.tensor.matmul(ps_h[:, 0:480], w["ident"][:, :], w["out1"][:, :], start=True, stop=True)
            with pe.Fori(1, BODIES) as i:
                for j in range(GPB):
                    hid(i, j)
                    edge_weights(i, j - 1)
                    sum_group(i, j - 2)
            edge_weights(BODIES, -1)
            sum_group(BODIES, -2)
            sum_group(BODIES, -1)

        @block.vector
        def _(dve):
            for c in (0, 1):
                nc.vector.memset(sums[:, c, :], 0.0).then_inc(prepared, 1)
            for j in range(GPB):
                nc.vector.memset(msg[j][:, :, 480:512], 0.0).then_inc(rows_free[j], 16)
            nc.vector.tensor_copy(iota, w["iota"][:, :]).then_inc(prepared, 1)
            dve.wait_ge(prepared, 5)
            dve.wait_ge(dst_in, 16)
            iota_t = iota.unsqueeze(1).broadcast_to([P, TPG, WIN])

            def rel_of(g):
                return dst_rel[:, bass.ds(g * TPG, TPG)]

            def add_group(i, o, earlier, count):
                g, j = GPB * i + o, o % GPB
                start = dve.value_load(w["table"][0:1, bass.ds(g, 1), 0:1], min_val=0, max_val=NPAD - 1)
                extras = dve.value_load(w["table"][0:1, bass.ds(g, 1), 1:2], min_val=0, max_val=NPAD // WIN - 1)
                window = ps_sum[j % 2][:, 0, 0:layer.chunks, :]
                dve.wait_ge(sum_done, g + 1)
                dve.wait_ge(earlier, count)
                at = sums[:, 0:layer.chunks, bass.ds(start, WIN)]
                nc.vector.tensor_tensor(at, at, window, ALU.add).then_inc(added, 1)
                with dve.If(extras):
                    before = dve.value_load(w["table"][0:1, bass.ds(g, 1), 2:3], min_val=0, max_val=G * (NPAD // WIN))
                    with dve.Fori(0, extras) as x:
                        dve.wait_ge(added, g + 1)
                        nc.vector.tensor_scalar(rel_of(g), rel_of(g), -float(WIN), None, ALU.add).then_inc(x_rel, 1)
                        dve.wait_ge(x_rel, before + x + 1)
                        nc.vector.tensor_tensor(match_x[:, :, :], iota_t, rel_of(g).unsqueeze(2).broadcast_to([P, TPG, WIN]),
                                                ALU.is_equal).then_inc(x_matched, 1)
                        dve.wait_ge(x_sum_done, before + x + 1)
                        there = nc.s_assert_within(
                            start + (x + 1) * WIN, 0, NPAD - 1,
                            skip_runtime_bounds_check_because="extras count the whole windows up to a destination below NPAD")
                        at = sums[:, 0:layer.chunks, bass.ds(there, WIN)]
                        nc.vector.tensor_tensor(at, at, window, ALU.add).then_inc(x_added, 1)
                        dve.wait_ge(x_added, before + x + 1)

            def messages(i, j):
                g, q, e0 = GPB * i + j, j // 2, (j % 2) * TPG
                if j % 2 == 0:
                    dve.wait_ge(attr_in[q], 16 * i + 16)
                    nc.vector.tensor_copy(e_p, attr[q][:, :, :]).then_inc(e_copied, 1)
                nc.vector.tensor_tensor(match[j % 2][:, :, :], iota_t, rel_of(g).unsqueeze(2).broadcast_to([P, TPG, WIN]),
                                        ALU.is_equal).then_inc(matched, 1)
                if j % 2 == 0:
                    dve.wait_ge(e_copied, 2 * i + q + 1)
                dve.wait_ge(gathered[j], GATHERED * i + GATHERED)
                r, m = rows[j], msg[j]

                def e3(c):
                    return e_p[:, e0:e0 + TPG, c:c + 3].unsqueeze(3).broadcast_to([P, TPG, 3, V])

                def comps(ap):
                    return ap.rearrange("p t (c n) -> p t c n", n=V)

                nc.vector.tensor_tensor(dots[:, :, :, :], e3(1), comps(r[:, :, 64:160]), ALU.mult).then_inc(own, 1)
                if L == 1:
                    nc.vector.tensor_tensor(comps(cross_a), e3(3), comps(r[:, :, 96:192]), ALU.mult).then_inc(own, 1)
                    nc.vector.tensor_tensor(comps(cross_b[:, :, :]), e3(2), comps(r[:, :, 128:224]), ALU.mult).then_inc(own, 1)
                for c in range(layer.act_comps, 3):
                    nc.vector.tensor_tensor(m[:, :, 64 * c:64 * c + 64],
                                            e_p[:, e0:e0 + TPG, c + 1:c + 2].broadcast_to([P, TPG, 64]),
                                            r[:, :, 0:64], ALU.mult).then_inc(own, 1)
                dve.wait_ge(own, layer.own * g + 1)
                nc.vector.tensor_reduce(m[:, :, 352:384], dots[:, :, :, :].rearrange("p t c n -> p t n c"),
                                        mybir.AxisListType.X, ALU.add).then_inc(own, 1)
                if L == 1:
                    dve.wait_ge(own, layer.own * g + 3)
                    nc.vector.tensor_tensor(m[:, :, 384:480], cross_a, cross_b[:, :, :], ALU.subtract).then_inc(own, 1)
                dve.wait_ge(w_done, g + 1)
                dve.wait_ge(act_parts, g + 1)
                wt = ps_w[j % 2][:, :].rearrange("p (t n) -> p t n", n=WPITCH)

                def times(c0, n, blocks, w0):
                    part = m[:, :, c0:c0 + n * blocks].rearrange("p t (c n) -> p t c n", n=n)
                    return nc.vector.tensor_tensor(part, wt[:, :, w0:w0 + n].unsqueeze(2).broadcast_to([P, TPG, blocks, n]),
                                                   part, ALU.mult)
                times(192, 64, 1, 0)
                times(256, 32, 3, 128)
                dve.wait_ge(own, layer.own * g + layer.own)
                times(0, 64, 3, 64).then_inc(rows_free[j], 16)
                last = times(352, 32, 1, 160)
                if L == 1:
                    last = times(384, 32, 3, 192)
                last.then_inc(msg_done, 1)

            for j in range(GPB):
                messages(0, j)
                if j >= 1:
                    add_group(0, j - 1, matched, j + 1)
            with dve.Fori(1, BODIES) as i:
                for j in range(GPB):
                    messages(i, j)
                    add_group(i, j - 1, matched, GPB * i + j + 1)
            add_group(BODIES, -1, added, G - 1)
            dve.wait_ge(added, G)


def layer0_nodes_phase(nc, d, w, sums):
    with ExitStack() as ctx:
        def sb(name, shape):
            return ctx.enter_context(nc.sbuf_tensor(f"m_{name}", shape, F32))

        def psum(name, shape):
            return ctx.enter_context(nc.psum_tensor(f"m_{name}", shape, F32))

        def sem(name):
            return ctx.enter_context(nc.semaphore(f"m_{name}"))

        R1 = D + V3 + S1
        x_v = [sb(f"xv{s}", [V3, TPU * P]) for s in range(UPB)]
        x_s = [sb(f"xs{s}", [S, TPU * P]) for s in range(UPB)]
        x_row = [sb(f"xrow{s}", [P, TPU, D]) for s in range(UPB)]
        x1 = [sb(f"x1_{s}", [P, TPU, D]) for s in range(UPB)]
        h1 = [sb(f"h1_{s}", [P, TPU, R1]) for s in range(UPB)]
        staged = [sb(f"staged{b}", [P, 3, P]) for b in range(2)]
        y = [[sb(f"y{b}_{c}", [P, D]) for c in range(4)] for b in range(2)]
        stats = [sb(f"stats{b}", [P, 6]) for b in range(2)]
        moments = [sb(f"moments{b}", [P, 2]) for b in range(2)]
        var = [sb(f"var{b}", [P, 1]) for b in range(2)]
        dev = [sb(f"dev{b}", [P, 1]) for b in range(2)]
        inv_dev = [sb(f"inv_dev{b}", [P, 1]) for b in range(2)]
        x1T_v = [sb(f"x1Tv{b}", [V3, P]) for b in range(2)]
        x1T_s = [sb(f"x1Ts{b}", [S, P]) for b in range(2)]
        ps_self = [psum(f"self{b}", [P, 512]) for b in range(2)]
        ps_agg = [psum(f"agg{b}", [P, 512]) for b in range(2)]
        ps_tr = [psum(f"tr{b}", [P, 512]) for b in range(2)]
        ps_next = [psum(f"next{b}", [P, 512]) for b in range(2)]

        loaded = [sem(f"loaded{s}") for s in range(UPB)]
        stored = [sem(f"stored{s}") for s in range(UPB)]
        stage_done, out_mm, chain, y_ready, statted, momented, var_ready = (
            sem(n) for n in ("stage_done", "out_mm", "chain", "y_ready", "statted", "momented", "var_ready"))
        dev_ready, inv_ready, x1_ready, tr_done, trs_copied, next_mm, h1_ready = (
            sem(n) for n in ("dev_ready", "inv_ready", "x1_ready", "tr_done", "trs_copied", "next_mm", "h1_ready"))
        block = ctx.enter_context(nc.Block())

        def pipeline(engine, stages):
            per = TPU * UPB

            def turn(i, j):
                for lag, step in stages:
                    if isinstance(i, int) and not 0 <= per * i + j - lag < NT:
                        continue
                    o = j - lag
                    body = i + o // per
                    step(per * i + o, body, (o % per) // TPU, o % TPU, o % 2)
            for j in range(per):
                turn(0, j)
            with engine.Fori(1, NBODY) as i:
                for j in range(per):
                    turn(i, j)
            for j in range(max(lag for lag, _ in stages)):
                turn(NBODY, j)

        @block.gpsimd
        def _(pool):
            def load(unit, i, s):
                at_least(pool, y_ready, TPU * unit - TPU)
                cols = bass.ds(unit * (TPU * P), TPU * P)
                pool.dma_start(x_v[s][:, :], d["xT_v"][:, cols]).then_inc(loaded[s], 16)
                pool.dma_start(x_s[s][:, :], d["xT_s"][:, cols]).then_inc(loaded[s], 16)
                pool.dma_start(x_row[s][:, :, :], d["x"][cols, :].rearrange("(k p) n -> p k n", p=P)).then_inc(loaded[s], 16)
            unit_loop(pool, load)

        @block.sync
        def _(sp):
            def store(unit, i, s):
                nodes = bass.ds(unit * (TPU * P), TPU * P)

                def rows(name):
                    return d[name][nodes, :].rearrange("(k p) n -> p k n", p=P)
                sp.wait_ge(x1_ready, TPU * unit + TPU)
                sp.dma_start(rows("x1"), x1[s][:, :, :]).then_inc(stored[s], 16)
                sp.wait_ge(h1_ready, TPU * unit + TPU)
                sp.dma_start(rows("table1")[:, :, 0:S], h1[s][:, :, V3:D]).then_inc(stored[s], 16)
                sp.dma_start(rows("table1")[:, :, S:D], h1[s][:, :, 0:V3]).then_inc(stored[s], 16)
                sp.dma_start(rows("table1")[:, :, D:D + 2 * V], h1[s][:, :, 0:2 * V]).then_inc(stored[s], 16)
                sp.dma_start(rows("self1"), h1[s][:, :, D:R1]).then_inc(stored[s], 16)
            unit_loop(sp, store)
            for s in range(UPB):
                sp.wait_ge(stored[s], 80 * NBODY)

        @block.scalar
        def _(act):
            def stage(n, i, s, k, b):
                at_least(act, out_mm, n - 1)
                nc.scalar.activation(staged[b][:, :, :], sums[:, 0:3, bass.ds(n * P, P)], ACT.Copy).then_inc(stage_done, 1)

            def deviation(n, i, s, k, b):
                act.wait_ge(var_ready, n + 1)
                at_least(act, inv_ready, n - 1)
                nc.scalar.activation(dev[b][:, :], var[b][:, :], ACT.Sqrt).then_inc(dev_ready, 1)

            def copy_transposed(n, i, s, k, b):
                act.wait_ge(tr_done, n + 1)
                at_least(act, next_mm, n - 1)
                nc.scalar.activation(x1T_v[b][:, :], ps_tr[b][0:V3, 0:P], ACT.Copy)
                nc.scalar.activation(x1T_s[b][:, :], ps_tr[b][0:S, P:2 * P], ACT.Copy).then_inc(trs_copied, 1)

            def scale_next(n, i, s, k, b):
                act.wait_ge(next_mm, n + 1)
                nc.scalar.activation(h1[s][:, k, :], ps_next[b][:, 0:R1], ACT.Copy,
                                     scale=w["attr"][:, bass.ds(n, 1), 0]).then_inc(h1_ready, 1)
            pipeline(act, ((0, stage), (3, deviation), (6, copy_transposed), (8, scale_next)))

        @block.tensor
        def _(pe):
            def output(n, i, s, k, b):
                if k == 0:
                    pe.wait_ge(loaded[s], 48 * i + 48)
                pe.wait_ge(stage_done, n + 1)
                at_least(pe, y_ready, n - 1)
                mine = ps_self[b][:, 0:2 * D].rearrange("p (a n) -> p a n", a=2)
                nc.tensor.matmul(mine[:, :, 0:V3], x_v[s][:, k * P:(k + 1) * P], w["node_v0"][:, 192:384], start=True, stop=True)
                nc.tensor.matmul(mine[:, :, V3:D], x_s[s][:, k * P:(k + 1) * P], w["node_s0"][:, 128:256], start=True, stop=True)
                agg = ps_agg[b][:, 0:2 * D].rearrange("p (a n) -> p a n", a=2)
                nc.tensor.matmul(agg, staged[b][:, 2, :], w["out0"][:, 0:320], start=True, stop=False)
                nc.tensor.matmul(agg[:, :, 0:64], staged[b][:, 0, :], w["out0"][:, 320:448], start=False, stop=False)
                nc.tensor.matmul(agg[:, :, 64:160], staged[b][:, 1, :], w["out0"][:, 448:640], start=False,
                                 stop=True).then_inc(out_mm, 1)

            def transpose(n, i, s, k, b):
                pe.wait_ge(x1_ready, n + 1)
                at_least(pe, trs_copied, n - 1)
                nc.tensor.transpose(ps_tr[b][0:V3, 0:P], x1[s][:, k, 0:V3], w["ident"][:, :])
                nc.tensor.transpose(ps_tr[b][0:S, P:2 * P], x1[s][:, k, V3:D], w["ident"][:, :]).then_inc(tr_done, 1)

            def next_layer(n, i, s, k, b):
                pe.wait_ge(trs_copied, n + 1)
                at_least(pe, h1_ready, n - 1)
                both = ps_next[b][:, 0:2 * D].rearrange("p (a n) -> p a n", a=2)
                nc.tensor.matmul(both[:, :, 0:V3], x1T_v[b][:, :], w["node_v1"][:, :], start=True, stop=True)
                nc.tensor.matmul(ps_next[b][:, V3:D], x1T_s[b][:, :], w["node_s1"][:, 0:64], start=True, stop=True)
                nc.tensor.matmul(ps_next[b][:, D + V3:R1], x1T_s[b][:, :], w["node_s1"][:, 64:160], start=True,
                                 stop=True).then_inc(next_mm, 1)
            pipeline(pe, ((1, output), (5, transpose), (7, next_layer)))

        @block.vector
        def _(dve):
            def residual(n, i, s, k, b):
                dve.wait_ge(out_mm, n + 1)
                if k == 0:
                    dve.wait_ge(loaded[s], 48 * i + 48)
                a, c = (w["attr"][:, bass.ds(n, 1), x] for x in range(2))
                am, cm = (w["masked"][:, bass.ds(n, 1), x] for x in range(2))
                terms = ((ps_self, 0, a), (ps_self, D, c), (ps_agg, 0, am), (ps_agg, D, cm))
                before = x_row[s][:, k, :]
                for x, (bank, c0, factor) in enumerate(terms):
                    if x:
                        dve.wait_ge(chain, 3 * n + x)
                    step = nc.vector.scalar_tensor_tensor(out=y[b][x][:, :], in0=bank[b][:, c0:c0 + D], scalar=factor,
                                                          in1=before, op0=ALU.mult, op1=ALU.add)
                    before = y[b][x][:, :]
                    step.then_inc(chain if x < 3 else y_ready, 1)
                dve.wait_ge(y_ready, n + 1)
                nc.vector.bn_stats(stats[b][:, :], y[b][3][:, :]).then_inc(statted, 1)
                dve.wait_ge(out_mm, 1)
                dve.wait_ge(statted, n + 1)
                nc.vector.bn_aggr(moments[b][:, :], stats[b][:, :]).then_inc(momented, 1)
                dve.wait_ge(momented, n + 1)
                at_least(dve, dev_ready, n - 1)
                nc.vector.tensor_scalar(var[b][:, :], moments[b][:, 1:2], EPS, None, ALU.add).then_inc(var_ready, 1)

            def normalize(n, i, s, k, b):
                dve.wait_ge(dev_ready, n + 1)
                nc.vector.reciprocal(inv_dev[b][:, :], dev[b][:, :]).then_inc(inv_ready, 1)
                dve.wait_ge(inv_ready, n + 1)
                if k == 0:
                    at_least(dve, stored[s], 80 * i)
                nc.vector.tensor_scalar(x1[s][:, k, :], y[b][3][:, :], moments[b][:, 0:1], inv_dev[b][:, :],
                                        ALU.subtract, ALU.mult).then_inc(x1_ready, 1)
            pipeline(dve, ((4, normalize), (2, residual)))


def layer1_nodes_phase(nc, d, w, sums):
    with ExitStack() as ctx:
        def sb(name, shape):
            return ctx.enter_context(nc.sbuf_tensor(f"f_{name}", shape, F32))

        def sem(name):
            return ctx.enter_context(nc.semaphore(f"f_{name}"))

        O1 = V3 + S1
        x_row = [sb(f"xrow{s}", [P, TPU, D]) for s in range(UPB)]
        self_row = [sb(f"self{s}", [P, TPU, O1]) for s in range(UPB)]
        staged = [sb(f"staged{b}", [P, 4, P]) for b in range(2)]
        pre = [sb(f"pre{b}", [P, O1]) for b in range(2)]
        silu = [sb(f"silu{b}", [P, S]) for b in range(2)]
        tanh = [sb(f"tanh{b}", [P, V]) for b in range(2)]
        gate = [sb(f"gate{b}", [P, V]) for b in range(2)]
        gated = [sb(f"gated{b}", [P, V3]) for b in range(2)]
        y = [sb(f"y{b}", [P, D]) for b in range(2)]
        centred = sb("centred", [P, NT, D])
        stats = [sb(f"stats{b}", [P, 6]) for b in range(2)]
        moments = [sb(f"moments{b}", [P, 2]) for b in range(2)]
        var, dev, inv_dev = sb("var", [P, NT]), sb("dev", [P, NT]), sb("inv_dev", [P, NT])
        ps = [ctx.enter_context(nc.psum_tensor(f"f_ps{b}", [P, 512], F32)) for b in range(2)]

        loaded = [sem(f"loaded{s}") for s in range(UPB)]
        stage_done, out_mm, pre_ready, acted, chain, y_ready, statted, momented = (
            sem(n) for n in ("stage_done", "out_mm", "pre_ready", "acted", "chain", "y_ready", "statted", "momented"))
        var_ready, dev_ready, inv_ready, normed, stored = (
            sem(n) for n in ("var_ready", "dev_ready", "inv_ready", "normed", "stored"))
        block = ctx.enter_context(nc.Block())

        @block.gpsimd
        def _(pool):
            def load(unit, i, s):
                at_least(pool, y_ready, TPU * unit - TPU)
                nodes = bass.ds(unit * (TPU * P), TPU * P)
                pool.dma_start(x_row[s][:, :, :], d["x1"][nodes, :].rearrange("(k p) n -> p k n", p=P)).then_inc(loaded[s], 16)
                pool.dma_start(self_row[s][:, :, :], d["self1"][nodes, :].rearrange("(k p) n -> p k n", p=P)
                               ).then_inc(loaded[s], 16)
            unit_loop(pool, load)

        @block.scalar
        def _(act):
            def stage(n, b):
                at_least(act, out_mm, n - 1)
                nc.scalar.activation(staged[b][:, :, :], sums[:, :, bass.ds(n * P, P)], ACT.Copy).then_inc(stage_done, 1)

            def gates(n, b):
                act.wait_ge(pre_ready, n + 1)
                at_least(act, y_ready, n - 1)
                nc.scalar.activation(silu[b][:, :], pre[b][:, V3:V3 + S], ACT.Silu)
                nc.scalar.activation(tanh[b][:, :], pre[b][:, V3 + S:O1], ACT.Tanh, scale=0.5).then_inc(acted, 1)

            stage(0, 0)

            def turn(n, unit, i, s, k):
                b = (TPU * s + k) % 2
                stage(n + 1, 1 - b)
                gates(n, b)
            for j in range(TPU * UPB):
                turn(j, 0, 0, j // TPU, j % TPU)
            with act.Fori(1, NBODY - 1) as i:
                for j in range(TPU * UPB):
                    turn(TPU * UPB * i + j, 0, i, j // TPU, j % TPU)
            for n in range(NT - TPU * UPB, NT):
                if n + 1 < NT:
                    stage(n + 1, (n + 1) % 2)
                gates(n, n % 2)
            act.wait_ge(var_ready, NT)
            nc.scalar.activation(dev[:, :], var[:, :], ACT.Sqrt).then_inc(dev_ready, 1)

        @block.tensor
        def _(pe):
            def output(n, unit, i, s, k):
                b = (TPU * s + k) % 2
                pe.wait_ge(stage_done, n + 1)
                at_least(pe, pre_ready, n - 1)
                o = ps[b]
                nc.tensor.matmul(o[:, 0:O1], staged[b][:, 2, :], w["out1"][:, 0:192], start=True, stop=False)
                nc.tensor.matmul(o[:, 0:64], staged[b][:, 0, :], w["out1"][:, 192:256], start=False, stop=False)
                nc.tensor.matmul(o[:, 64:O1], staged[b][:, 1, :], w["out1"][:, 256:384], start=False, stop=False)
                nc.tensor.matmul(o[:, 0:V3], staged[b][:, 3, :], w["out1"][:, 384:480], start=False, stop=True).then_inc(out_mm, 1)
            node_loop(pe, output)

        @block.vector
        def _(dve):
            def before_gates(n, i, s, k, b):
                dve.wait_ge(out_mm, n + 1)
                if k == 0:
                    dve.wait_ge(loaded[s], 32 * i + 32)
                at_least(dve, acted, n - 1)
                nc.vector.scalar_tensor_tensor(out=pre[b][:, :], in0=ps[b][:, 0:O1], scalar=w["attr"][:, bass.ds(n, 1), 0],
                                               in1=self_row[s][:, k, :], op0=ALU.mult, op1=ALU.add).then_inc(pre_ready, 1)

            def after_gates(n, i, s, k, b):
                dve.wait_ge(acted, n + 1)
                nc.vector.tensor_scalar(gate[b][:, :], tanh[b][:, :], 1.0, 0.5, ALU.add, ALU.mult).then_inc(chain, 1)
                nc.vector.tensor_tensor(y[b][:, V3:D], silu[b][:, :], x_row[s][:, k, V3:D], ALU.add)
                dve.wait_ge(chain, 2 * n + 1)
                nc.vector.tensor_tensor(gated[b][:, :].rearrange("p (c n) -> p c n", n=V),
                                        pre[b][:, 0:V3].rearrange("p (c n) -> p c n", n=V),
                                        gate[b][:, :].unsqueeze(1).broadcast_to([P, 3, V]), ALU.mult).then_inc(chain, 1)
                dve.wait_ge(chain, 2 * n + 2)
                nc.vector.tensor_tensor(y[b][:, 0:V3], gated[b][:, :], x_row[s][:, k, 0:V3], ALU.add).then_inc(y_ready, 1)
                dve.wait_ge(y_ready, n + 1)
                nc.vector.bn_stats(stats[b][:, :], y[b][:, :]).then_inc(statted, 1)
                dve.wait_ge(out_mm, 1)
                dve.wait_ge(statted, n + 1)
                nc.vector.bn_aggr(moments[b][:, :], stats[b][:, :]).then_inc(momented, 1)
                dve.wait_ge(momented, n + 1)
                nc.vector.tensor_scalar(centred[:, bass.ds(n, 1), :], y[b][:, :].unsqueeze(1), moments[b][:, 0:1], None, ALU.subtract)
                nc.vector.tensor_scalar(var[:, bass.ds(n, 1)], moments[b][:, 1:2], EPS, None, ALU.add).then_inc(var_ready, 1)

            before_gates(0, 0, 0, 0, 0)
            per = TPU * UPB

            def turn(i, j):
                o = j + 1
                before_gates(per * i + o, i + o // per, (o % per) // TPU, o % TPU, o % 2)
                after_gates(per * i + j, i, j // TPU, j % TPU, j % 2)
            for j in range(per):
                turn(0, j)
            with dve.Fori(1, NBODY - 1) as i:
                for j in range(per):
                    turn(i, j)
            for j in range(per - 1):
                turn(NBODY - 1, j)
            after_gates(NT - 1, NBODY - 1, UPB - 1, TPU - 1, (NT - 1) % 2)

            dve.wait_ge(dev_ready, 1)
            nc.vector.reciprocal(inv_dev[:, :], dev[:, :]).then_inc(inv_ready, 1)
            dve.wait_ge(inv_ready, 1)
            with dve.Fori(0, NT // TPU) as u:
                for k in range(TPU):
                    row = centred[:, bass.ds(u * TPU + k, 1), :]
                    nc.vector.tensor_scalar(row, row, inv_dev[:, bass.ds(u * TPU + k, 1)], None, ALU.mult).then_inc(normed, 1)

        @block.sync
        def _(sp):
            with sp.Fori(0, NT // TPU) as u:
                sp.wait_ge(normed, TPU * u + TPU)
                sp.dma_start(d["out"][bass.ds(u * (TPU * P), TPU * P), :].rearrange("(k p) n -> p k n", p=P),
                             centred[:, bass.ds(u * TPU, TPU), :]).then_inc(stored, 16)
            sp.wait_ge(stored, 16 * (NT // TPU))


INPUTS = (
    ("x", (NPAD, D), F32), ("xT_v", (V3, NPAD), F32), ("xT_s", (S, NPAD), F32), ("attr", (P, NT, 3), F32),
    ("src", (P, T), I32), ("dst_tile", (P, T), I32), ("dst_by_group", (GP, GQ, GE), I32),
    ("edge_attr", (P, T, 6), F32), ("inputs0", (NB0, EPAD), F32), ("inputs1", (2 * NB1, EPAD // 2), F32),
    ("fc1_0", (NB0, H0), F32), ("fc2_0", (H0, 192), F32), ("fc1_1", (P, P), F32), ("fc2_1", (P, 480), F32),
    ("node_s0", (S, 256), F32), ("node_v0", (V3, 384), F32), ("node_s1", (S, 160), F32), ("node_v1", (V3, 192), F32),
    ("out1", (P, 480), F32), ("l2", (MID, 16, P), F32), ("l3", (MID, S + V), F32),
)
SCRATCH = (
    ("table0", (NPAD, D), F32), ("table1", (NPAD, D + 2 * V), F32), ("x1", (NPAD, D), F32), ("self1", (NPAD, V3 + S1), F32),
    ("lo_dram", (G,), I32), ("extra_dram", (G,), I32), ("dst_rel", (P, T), F32),
)


def build(nc):
    d = {name: nc.dram_tensor("in_" + name, shape, dt, kind="ExternalInput").ap() for name, shape, dt in INPUTS}
    d["out"] = nc.dram_tensor("out", (NPAD, D), F32, kind="ExternalOutput").ap()
    for name, shape, dt in SCRATCH:
        d[name] = nc.dram_tensor("scratch_" + name, shape, dt).ap()
    with ExitStack() as ctx:
        w = kept_tensors(nc, ctx)
        setup_phase(nc, d, w)
        sums = ctx.enter_context(nc.sbuf_tensor("sums", [P, 4, SUMW], F32))
        edge_phase(nc, d, w, sums, Layer(0))
        layer0_nodes_phase(nc, d, w, sums)
        edge_phase(nc, d, w, sums, Layer(1))
        layer1_nodes_phase(nc, d, w, sums)


def lay_out(inputs):
    a = {k: np.asarray(v) for k, v in inputs.items()}
    f = np.float32

    def padded(v, n, fill=0):
        out = np.full((n,) + v.shape[1:], fill, v.dtype)
        out[:v.shape[0]] = v
        return out

    def by_partition(v):
        return np.ascontiguousarray(np.swapaxes(v.reshape((-1, P) + v.shape[1:]), 0, 1))

    def diagonal(*blocks):
        out = np.zeros((V3, V3 * len(blocks)), f)
        for k, block in enumerate(blocks):
            for c in range(3):
                out[V * c:V * c + V, V3 * k + V * c:V3 * k + V * c + V] = block
        return out

    x = padded(a["x"], NPAD)
    xv = x[:, S:].reshape(NPAD, V, 3).transpose(0, 2, 1).reshape(NPAD, V3)
    r = {"x": np.concatenate([xv, x[:, :S]], 1), "xT_v": xv.T.copy(), "xT_s": x[:, :S].T.copy()}
    r["attr"] = by_partition(padded(np.concatenate([a["node_vec1"], a["node_vec1_n2"], a["node_vec1_n3"]], 1), NPAD))
    r["src"] = by_partition(padded(a["src"], EPAD))
    dst = padded(a["dst"], EPAD, NPAD - 1)
    r["dst_tile"] = by_partition(dst)
    r["dst_by_group"] = dst.reshape(GP, GQ, GE)
    e = padded(a["edge_attr_4"], EPAD)
    r["edge_attr"] = by_partition(np.concatenate([e, e[:, 1:3]], 1))
    r["inputs0"] = padded(a["edge_attr_10"], EPAD).T.copy()
    r["inputs1"] = padded(a["edge_attr_64"], EPAD).reshape(T // 2, 2, P, NB1).transpose(1, 3, 0, 2).reshape(2 * NB1, EPAD // 2)
    L0 = {k[7:]: v for k, v in a.items() if k.startswith("L0_gnn_")}
    L1 = {k[7:]: v for k, v in a.items() if k.startswith("L1_gnn_")}
    r["fc1_0"], r["fc2_0"] = L0["W_fc1"], L0["W_fc2"]
    r["fc1_1"] = np.zeros((P, P), f)
    r["fc1_1"][:H1, :H1] = r["fc1_1"][H1:, H1:] = L1["fc_w1"]
    r["fc2_1"] = np.zeros((P, 480), f)
    r["fc2_1"][:H1, :224] = r["fc2_1"][H1:, WPITCH:] = L1["fc_w2"]
    names = ("l1_a", "l1_c", "sc_a", "sc_c")
    r["node_s0"] = np.concatenate([L0["Ws_" + n] for n in names], 1)
    r["node_v0"] = diagonal(*(L0["Wv_" + n] for n in names))
    r["node_s1"] = np.concatenate([L1["lin1_ws"], L1["sc_ws"]], 1)
    r["node_v1"] = diagonal(L1["lin1_wv"], L1["sc_wv"])
    v, s, o = L1["lin2_wv"], L1["lin2_ws"], np.zeros((P, 480), f)
    for c in range(3):
        o[V * c:V * c + V, V * c:V * c + V] = v[64:96]
        o[V * c:V * c + V, 384 + V * c:384 + V * c + V] = v[96:128]
    o[96:128, 96:192] = s[64:96]
    o[0:64, 192:224] = o[64:128, 224:256] = o[0:64, 256:288] = v[0:64]
    o[64:128, 288:384] = s[0:64]
    r["out1"] = o
    l2 = np.zeros((MID, 16, P), f)
    for k, attr in enumerate("ac"):
        sT, vT = L0["Ws_l2_" + attr].T, L0["Wv_l2_" + attr].T
        for c in range(3):
            l2[:, 3 * k + c, V * c:V * c + V] = vT[:, 64:96]
        l2[:, 6 + k, 96:128] = sT[:, 64:96]
        l2[:, 8 + 2 * k, 0:64] = l2[:, 9 + 2 * k, 64:128] = vT[:, 0:64]
        l2[:, 12 + k, 0:64] = vT[:, 0:64]
        l2[:, 14 + k, 64:128] = sT[:, 0:64]
    r["l2"] = l2
    r["l3"] = np.concatenate([L0["Ws_l3"], L0["Wv_l3"]], 1)
    return {"in_" + k: np.ascontiguousarray(v) for k, v in r.items()}


def kernel(**inputs):
    import concourse.bacc as bacc
    from concourse.bass_utils import run_bass_kernel_spmd

    nc = bacc.Bacc("TRN2", target_bir_lowering=False, num_devices=1)
    build(nc)
    out = run_bass_kernel_spmd(nc, [lay_out(inputs)], core_ids=[0]).results[0]["out"][:NODES]
    vectors = out[:, :V3].reshape(NODES, 3, V).transpose(0, 2, 1).reshape(NODES, V3)
    return np.concatenate([out[:, V3:], vectors], 1)
```

```python
from contextlib import ExitStack

import numpy as np
import concourse.bass as bass
from concourse import mybir

F32 = mybir.dt.float32
I32 = mybir.dt.int32
ALU = mybir.AluOpType
ACT = mybir.ActivationFunctionType

P = 128
NODES, EDGES = 6250, 200000
S, V = 64, 32
V3 = 3 * V
D = V3 + S
NB0, H0 = 10, 100
NB1, H1 = 64, 64
MID = 96
S1 = 96

TPU, UPB = 5, 2
NBODY = 5
NT = TPU * UPB * NBODY
NPAD = NT * P
assert NPAD > NODES and (TPU * UPB) % 2 == 0

TPG = 4
GE = TPG * P
GPB = 4
BODIES = -(-EDGES // (GE * GPB))
G = BODIES * GPB
EPAD = G * GE
T = G * TPG
WIN = 40
assert WIN == 40 and all(((n >> 3) * 205) >> 10 == n // WIN for n in range(NPAD))
SUMW = NPAD + WIN
GQ = 4
GP = G // GQ
assert GP * GQ == G and GP <= P
TAB = 4
EXTRA_BITS = 8
assert NPAD // WIN - 1 < 1 << EXTRA_BITS
WPITCH = 256
MW = 448
WARM_UP = 5
AHEAD = 2
MSG0 = 16
GATHERED = 16 * TPG

C_S, C_X = float(np.sin(np.pi / 8)), float(np.cos(np.pi / 8))
INV_NN = 0.25
EPS = 1e-5
R3, R2 = 1 / float(np.sqrt(3)), 1 / float(np.sqrt(2))


class Layer:

    def __init__(self, index):
        self.index = index
        self.row = 160 if index == 0 else 224
        self.act_scales = 3 if index == 0 else 4
        self.chunks = 3 if index == 0 else 4
        self.tiles_per_product = 1 if index == 0 else 2
        self.kin = NB0 if index == 0 else 2 * NB1
        self.hid = H0 if index == 0 else 2 * H1
        self.group_cols = GE // self.tiles_per_product
        self.silu_scale = 1.0 if index == 0 else 1 / float(np.sqrt(NB1))


def kept_tensors(nc, ctx):
    w = {}
    for name, shape, dt in (
        ("fc1_0", [P, H0], F32), ("fc2_0", [H0, 192], F32), ("fc1_1", [P, P], F32), ("fc2_1", [P, 480], F32),
        ("node_s0", [S, 256], F32), ("node_v0", [V3, 384], F32), ("node_s1", [S, 160], F32), ("node_v1", [V3, 192], F32),
        ("out0", [P, 640], F32), ("out1", [P, 480], F32), ("ident", [P, P], F32), ("iota", [P, WIN], F32),
        ("attr", [P, NT, 3], F32), ("masked", [P, NT, 2], F32), ("table", [1, G, TAB], I32),
    ):
        w[name] = ctx.enter_context(nc.sbuf_tensor("k_" + name, shape, dt))
    return w


def node_loop(engine, step):
    for j in range(TPU * UPB):
        step(j, j // TPU, 0, j // TPU, j % TPU)
    with engine.Fori(1, NBODY) as i:
        for j in range(TPU * UPB):
            step(TPU * UPB * i + j, UPB * i + j // TPU, i, j // TPU, j % TPU)


def unit_loop(engine, step):
    for s in range(UPB):
        step(s, 0, s)
    with engine.Fori(1, NBODY) as i:
        for s in range(UPB):
            step(UPB * i + s, i, s)


def at_least(engine, sem, value):
    if not (isinstance(value, int) and value <= 0):
        engine.wait_ge(sem, value)


def setup_phase(nc, d, w, sums):
    with ExitStack() as ctx:
        def sb(name, shape, dt=F32):
            return ctx.enter_context(nc.sbuf_tensor(name, shape, dt))

        def sem(name):
            return ctx.enter_context(nc.semaphore(name))

        x_v = [sb(f"s_xv{i}", [V3, TPU * P]) for i in range(UPB)]
        x_s = [sb(f"s_xs{i}", [S, TPU * P]) for i in range(UPB)]
        l2 = sb("s_l2", [MID, 16, P])
        l3 = sb("s_l3", [MID, S + V])
        dst_by_group = sb("dst_by_group", [GP, GQ, GE], I32)
        dst_by_group_f = sb("dst_by_group_f", [GP, GQ, GE])
        lo_f, hi_f, span_f = sb("lo_f", [GP, GQ]), sb("hi_f", [GP, GQ]), sb("span_f", [GP, GQ])
        span_i, lo_i, extra_i = (sb(n, [GP, GQ], I32) for n in ("span_i", "lo_i", "extra_i"))
        lo_row, extra_row, before_row = (sb(n, [1, G], I32) for n in ("lo_row", "extra_row", "before_row"))
        scan = [sb(f"scan{i}", [1, G]) for i in range(2)]
        lo_all = sb("lo_all", [P, G], I32)
        lo_all_f = sb("lo_all_f", [P, G])
        dst_tile = sb("dst_tile_i", [P, T], I32)
        dst_rel = sb("dst_rel_new", [P, T])
        iota_i = sb("iota_i", [P, WIN], I32)
        part_a = [sb(f"part_a{i}", [P, D]) for i in range(2)]
        h0 = [sb(f"h0_{i}", [P, TPU, D]) for i in range(UPB)]
        ps_out = ctx.enter_context(nc.psum_tensor("ps_out", [P, 1024], F32))
        ps_node = [ctx.enter_context(nc.psum_tensor(f"s_psn{i}", [P, 512], F32)) for i in range(2)]

        weights_in, l_in, attr_in, dst_in, dtile_in = (sem(n) for n in ("weights_in", "l_in", "attr_in", "dst_in", "dtile_in"))
        pool_made = sem("pool_made")
        out0_done = sem("out0_done")
        scaled = sem("scaled")
        masked_done = sem("masked_done")
        grp = sem("grp")
        tab_out, tab_in, rel_out = sem("tab_out"), sem("tab_in"), sem("rel_out")
        x_in = [sem(f"s_x_in{i}") for i in range(UPB)]
        node_mm, part_ready, h_ready = sem("s_node_mm"), sem("s_part_ready"), sem("s_h_ready")
        h_out = [sem(f"s_h_out{i}") for i in range(UPB)]
        block = ctx.enter_context(nc.Block())

        SCALES = (
            ("node_s0", 128, 256, C_S), ("node_v0", 192, 384, C_S),
            ("fc2_0", 0, 160, INV_NN), ("fc2_0", 160, 192, INV_NN * R3),
            *(("fc2_1", c0 + WPITCH * k, c1 + WPITCH * k, factor) for k in range(2) for c0, c1, factor in (
                (0, 160, INV_NN / 8), (160, 192, INV_NN / 8 * R3), (192, 224, INV_NN / 8 * R2))),
            ("node_s1", 0, 160, 1 / 8), ("node_v1", 0, 192, 1 / float(np.sqrt(V))),
            ("out1", 0, 96, 1 / float(np.sqrt(128))), ("out1", 96, 192, 1 / float(np.sqrt(96))),
            ("out1", 192, 288, 1 / float(np.sqrt(128))), ("out1", 288, 384, 1 / float(np.sqrt(96))),
            ("out1", 384, 480, 1 / float(np.sqrt(128))),
        )
        DIRECT = ("node_v0", "node_s0", "fc1_0", "fc2_0", "fc1_1", "fc2_1", "node_s1", "node_v1", "out1")

        @block.sync
        def _(sp):
            for name in DIRECT:
                sp.dma_start(w[name][:, :], d[name]).then_inc(weights_in, 16)
            sp.dma_start(l2[:, :, :], d["l2"]).then_inc(l_in, 16)
            sp.dma_start(l3[:, :], d["l3"]).then_inc(l_in, 16)
            sp.wait_ge(grp, 8)
            sp.dma_start(d["lo_dram"].rearrange("(p q) -> p q", q=GQ), lo_i[:, :]).then_inc(tab_out, 16)
            sp.dma_start(d["extra_dram"].rearrange("(p q) -> p q", q=GQ), extra_i[:, :]).then_inc(tab_out, 16)
            sp.wait_ge(tab_out, 32)
            lo_line = d["lo_dram"].rearrange("(a g) -> a g", a=1)
            sp.dma_start(lo_all[:, :], lo_line.broadcast_to([P, G])).then_inc(tab_in, 16)
            sp.dma_start(lo_row[:, :], lo_line).then_inc(tab_in, 16)
            sp.dma_start(extra_row[:, :], d["extra_dram"].rearrange("(a g) -> a g", a=1)).then_inc(tab_in, 16)
            sp.wait_ge(grp, 11)
            sp.dma_start(d["dst_rel"], dst_rel[:, :]).then_inc(rel_out, 16)

            def store(unit, i, s):
                sp.wait_ge(h_ready, TPU * unit + TPU)
                rows = d["table0"][bass.ds(unit * (TPU * P), TPU * P), :].rearrange("(k p) n -> p k n", p=P)
                sp.dma_start(rows[:, :, 0:S], h0[s][:, :, V3:D]).then_inc(h_out[s], 16)
                sp.dma_start(rows[:, :, S:D], h0[s][:, :, 0:V3]).then_inc(h_out[s], 16)
            unit_loop(sp, store)
            for s in range(UPB):
                sp.wait_ge(h_out[s], 32 * NBODY)
            sp.wait_ge(rel_out, 16)

        @block.gpsimd
        def _(pool):
            nc.gpsimd.iota(iota_i[:, :], [[1, WIN]], base=0, channel_multiplier=0).then_inc(pool_made, 1)
            nc.gpsimd.memset(w["ident"][:, :], 0.0).then_inc(pool_made, 1)
            pool.wait_ge(pool_made, 2)
            nc.gpsimd.affine_select(out=w["ident"][:, :], in_=w["ident"][:, :], compare_op=ALU.not_equal, fill=1.0,
                                    base=0, pattern=[[-1, P]], channel_multiplier=1).then_inc(pool_made, 1)

            def load(unit, i, s):
                at_least(pool, node_mm, TPU * unit - TPU)
                cols = bass.ds(unit * (TPU * P), TPU * P)
                pool.dma_start(x_v[s][:, :], d["xT_v"][:, cols]).then_inc(x_in[s], 16)
                pool.dma_start(x_s[s][:, :], d["xT_s"][:, cols]).then_inc(x_in[s], 16)
            for s in range(UPB):
                load(s, 0, s)
            nc.gpsimd.memset(sums[:, :, :], 0.0)
            with pool.Fori(1, NBODY) as i:
                for s in range(UPB):
                    load(UPB * i + s, i, s)

        @block.scalar
        def _(act):
            act.dma_start(w["attr"][:, :, :], d["attr"]).then_inc(attr_in, 16)
            act.dma_start(dst_by_group[:, :, :], d["dst_by_group"]).then_inc(dst_in, 16)
            act.dma_start(dst_tile[:, :], d["dst_tile"]).then_inc(dtile_in, 16)
            act.wait_ge(attr_in, 16)

            def part(n, unit, i, s, k):
                act.wait_ge(node_mm, n + 1)
                at_least(act, h_ready, n - 1)
                nc.scalar.activation(part_a[(TPU * s + k) % 2][:, :],
                                     ps_node[(TPU * s + k) % 2][:, 0:D], ACT.Copy,
                                     scale=w["attr"][:, bass.ds(n, 1), 0]).then_inc(part_ready, 1)
            node_loop(act, part)

        @block.tensor
        def _(pe):
            pe.wait_ge(l_in, 32)
            for c in range(16):
                vec = c not in (6, 7, 14, 15)
                col = OUT0_COLUMNS[c] + (64 if c >= 12 else 0)
                n = V if vec else S
                last = nc.tensor.matmul(ps_out[:, col:col + n], l2[:, c, :], l3[:, S:S + V] if vec else l3[:, 0:S],
                                        start=True, stop=True)
            last.then_inc(out0_done, 1)
            pe.wait_ge(weights_in, 16 * len(DIRECT))

            def project(n, unit, i, s, k):
                if k == 0:
                    pe.wait_ge(x_in[s], 32 * i + 32)
                at_least(pe, h_ready, n - 1)
                out = ps_node[(TPU * s + k) % 2][:, 0:2 * D].rearrange("p (a n) -> p a n", a=2)
                nc.tensor.matmul(out[:, :, 0:V3], x_v[s][:, k * P:(k + 1) * P], w["node_v0"][:, 0:192], start=True, stop=True)
                nc.tensor.matmul(out[:, :, V3:D], x_s[s][:, k * P:(k + 1) * P], w["node_s0"][:, 0:128],
                                 start=True, stop=True).then_inc(node_mm, 1)
            node_loop(pe, project)

        @block.vector
        def _(dve):
            dve.wait_ge(dst_in, 16)
            nc.vector.tensor_scalar(dst_by_group_f[:, :, :], dst_by_group[:, :, :], float(NPAD - 1), None, ALU.min).then_inc(grp, 1)
            dve.wait_ge(grp, 1)
            nc.vector.tensor_reduce(lo_f[:, :], dst_by_group_f[:, :, :], mybir.AxisListType.X, ALU.min)
            nc.vector.tensor_reduce(hi_f[:, :], dst_by_group_f[:, :, :], mybir.AxisListType.X, ALU.max).then_inc(grp, 1)
            dve.wait_ge(grp, 2)
            nc.vector.tensor_copy(lo_i[:, :], lo_f[:, :]).then_inc(grp, 1)
            nc.vector.tensor_tensor(span_f[:, :], hi_f[:, :], lo_f[:, :], ALU.subtract).then_inc(grp, 1)
            dve.wait_ge(grp, 4)
            nc.vector.tensor_copy(span_i[:, :], span_f[:, :]).then_inc(grp, 1)
            dve.wait_ge(grp, 5)
            nc.vector.tensor_scalar(span_i[:, :], span_i[:, :], 3, None, ALU.arith_shift_right).then_inc(grp, 1)
            dve.wait_ge(grp, 6)
            nc.vector.tensor_scalar(span_i[:, :], span_i[:, :], 205, None, ALU.mult).then_inc(grp, 1)
            dve.wait_ge(grp, 7)
            nc.vector.tensor_scalar(extra_i[:, :], span_i[:, :], 10, None, ALU.arith_shift_right).then_inc(grp, 1)

            dve.wait_ge(weights_in, 16 * len(DIRECT))
            for name, c0, c1, factor in SCALES[:2]:
                nc.vector.tensor_scalar(w[name][:, c0:c1], w[name][:, c0:c1], factor, None, ALU.mult)
            dve.wait_ge(attr_in, 16)

            def add_c(n, unit, i, s, k):
                dve.wait_ge(part_ready, n + 1)
                if k == 0:
                    at_least(dve, h_out[s], 32 * i)
                nc.vector.scalar_tensor_tensor(
                    out=h0[s][:, k, :], in0=ps_node[(TPU * s + k) % 2][:, D:2 * D], scalar=w["attr"][:, bass.ds(n, 1), 1],
                    in1=part_a[(TPU * s + k) % 2][:, :], op0=ALU.mult, op1=ALU.add).then_inc(h_ready, 1)

            dve.wait_ge(tab_in, 48)
            dve.wait_ge(dtile_in, 16)
            nc.vector.tensor_copy(lo_all_f[:, :], lo_all[:, :])
            nc.vector.tensor_scalar(dst_rel[:, :], dst_tile[:, :], float(NPAD - 1), None, ALU.min).then_inc(grp, 1)
            dve.wait_ge(grp, 9)
            rel = dst_rel[:, :].rearrange("p (g t) -> p g t", t=TPG)
            nc.vector.tensor_tensor(rel, rel, lo_all_f[:, :].unsqueeze(2).broadcast_to([P, G, TPG]), ALU.subtract).then_inc(grp, 1)
            nc.vector.tensor_copy(scan[0][:, :], extra_row[:, :]).then_inc(grp, 1)
            node_loop(dve, add_c)

            count = 11
            shift, n = 1, 0
            while shift < G:
                a, b = scan[n % 2], scan[(n + 1) % 2]
                dve.wait_ge(grp, count)
                nc.vector.tensor_copy(b[:, 0:shift], a[:, 0:shift])
                nc.vector.tensor_tensor(b[:, shift:G], a[:, shift:G], a[:, 0:G - shift], ALU.add).then_inc(grp, 1)
                shift, n, count = 2 * shift, n + 1, count + 1
            dve.wait_ge(grp, count)
            nc.vector.tensor_tensor(before_row[:, :], scan[n % 2][:, :], extra_row[:, :], ALU.subtract).then_inc(grp, 1)
            dve.wait_ge(grp, count + 1)
            nc.vector.scalar_tensor_tensor(out=w["table"][:, :, 0], in0=lo_row[:, :], scalar=float(1 << EXTRA_BITS),
                                           in1=extra_row[:, :], op0=ALU.mult, op1=ALU.add)
            for c, row in ((1, extra_row), (2, before_row)):
                nc.vector.tensor_copy(w["table"][:, :, c], row[:, :])
            nc.vector.memset(w["table"][:, :, 3], 0)

            for name, c0, c1, factor in SCALES[2:]:
                nc.vector.tensor_scalar(w[name][:, c0:c1], w[name][:, c0:c1], factor, None, ALU.mult)
            dve.wait_ge(out0_done, 1)
            nc.vector.tensor_scalar(w["out0"][:, 0:448], ps_out[:, 0:448], C_X, None, ALU.mult)
            nc.vector.tensor_scalar(w["out0"][:, 448:640], ps_out[:, 512:704], C_X, None, ALU.mult)
            for c in range(2):
                nc.vector.tensor_tensor(w["masked"][:, :, c], w["attr"][:, :, c], w["attr"][:, :, 2], ALU.mult)
            dve.wait_ge(pool_made, 3)
            nc.vector.tensor_copy(w["iota"][:, :], iota_i[:, :]).then_inc(scaled, 1)
            dve.wait_ge(scaled, 1)


OUT0_COLUMNS = [0, 32, 64, 160, 192, 224, 96, 256, 320, 352, 384, 416, 448, 544, 480, 576]


def edge_phase(nc, d, w, sums, layer):
    L = layer.index
    table_dram = d[f"table{L}"]
    with ExitStack() as ctx:
        def sb(name, shape, dt=F32):
            return ctx.enter_context(nc.sbuf_tensor(f"e{L}_{name}", shape, dt))

        def psum(name, shape):
            return ctx.enter_context(nc.psum_tensor(f"e{L}_{name}", shape, F32))

        def sem(name):
            return ctx.enter_context(nc.semaphore(f"e{L}_{name}"))

        index = [sb(f"index{q}", [P, 2 * TPG], I32) for q in range(2)]
        attr = [sb(f"attr{q}", [P, 2 * TPG, 6]) for q in range(2)]
        inputs = [sb(f"inputs{q}", [P, 2 * layer.group_cols]) for q in range(2)]
        rows = [sb(f"rows{j}", [P, TPG, layer.row]) for j in range(GPB)]
        msg = [sb(f"msg{b}", [P, TPG, MW]) for b in range(2)]
        hidden = [sb(f"hidden{b}", [layer.hid, layer.group_cols]) for b in range(2)]
        cross_b = sb("cross_b", [P, TPG, V3])
        match = [sb(f"match{j}", [P, TPG, 5, WIN]) for j in range(GPB)]
        match_x = sb("match_x", [P, TPG, 5, WIN])
        e_kept = [sb(f"e_kept{q}", [P, 2 * TPG, 6]) for q in range(2)]
        dst_rel = sb("dst_rel", [P, T + AHEAD * TPG])

        ps_w = [psum(f"w{b}", [P, TPG * WPITCH]) for b in range(2)]
        ps_h = psum("h", [P, GE])
        ps_sum = [psum(f"sum{b}", [P, 512])[:, 0:4 * WIN].rearrange("p (c n) -> p c n", n=WIN) for b in range(2)]
        ps_misc = psum("misc", [P, 512])
        iota = ps_misc[:, 0:WIN]
        e_p = ps_misc[:, 64:112].rearrange("p (t c) -> p t c", c=6)
        cross_a = ps_misc[:, 112:496].rearrange("p (t n) -> p t n", t=TPG)

        prepared, zeroed, dst_in = sem("prepared"), sem("zeroed"), sem("dst_in")
        index_in = [sem(f"index_in{q}") for q in range(2)]
        attr_in = [sem(f"attr_in{q}") for q in range(2)]
        inputs_in = [sem(f"inputs_in{q}") for q in range(2)]
        gathered = [sem(f"gathered{j}") for j in range(GPB)]
        msg_done = [sem(f"msg_done{j}") for j in range(GPB)]
        hid_done, silu_done, w_done = sem("hid_done"), sem("silu_done"), sem("w_done")
        e_copied, crossed, subtracted, scaled = sem("e_copied"), sem("crossed"), sem("subtracted"), sem("scaled")
        matched = sem("matched")
        sum_done, added = sem("sum_done"), sem("added")
        x_rel, x_matched, x_sum_done, x_added = sem("x_rel"), sem("x_matched"), sem("x_sum_done"), sem("x_added")
        block = ctx.enter_context(nc.Block())

        def group_loop(engine, step):
            for j in range(GPB):
                step(0, j)
            with engine.Fori(1, BODIES) as i:
                for j in range(GPB):
                    step(i, j)

        @block.sync
        def _(sp):
            def load(i, q):
                tiles = bass.ds((2 * i + q) * (2 * TPG), 2 * TPG)
                if not isinstance(i, int):
                    for j in (2 * q, 2 * q + 1):
                        sp.wait_ge(gathered[j], GATHERED * i)
                sp.dma_start(index[q][:, :], d["src"][:, tiles]).then_inc(index_in[q], 16)
                if not isinstance(i, int):
                    sp.wait_ge(hid_done, GPB * i - GPB + 2 * q + 2)
                cols = 2 * layer.group_cols
                if L == 0 and isinstance(i, int):
                    sp.wait_ge(zeroed, 2)
                sp.dma_start(inputs[q][0:layer.kin, :], d[f"inputs{L}"][:, bass.ds((2 * i + q) * cols, cols)]).then_inc(inputs_in[q], 16)
                if not isinstance(i, int):
                    sp.wait_ge(sum_done, GPB * i - GPB + 2 * q + 2)
                sp.dma_start(attr[q][:, :, :], d["edge_attr"][:, tiles, :]).then_inc(attr_in[q], 16)
            load(0, 0)
            sp.dma_start(dst_rel[:, 0:T], d["dst_rel"]).then_inc(dst_in, 16)
            load(0, 1)
            with sp.Fori(1, BODIES) as i:
                for q in range(2):
                    load(i, q)

        @block.gpsimd
        def _(pool):
            def gather(count, j):
                q = j // 2
                pool.wait_ge(prepared, 1)
                pool.wait_ge(index_in[q], count)
                pool.wait_ge(msg_done[j], count)
                for t in range(TPG):
                    c = (j % 2) * TPG + t
                    pool.indirect_dma_start(
                        out=rows[j][:, t, :], out_offset=None, in_=table_dram,
                        in_offset=bass.IndirectOffsetOnAxis(ap=index[q][:, c:c + 1], axis=0),
                    ).then_inc(gathered[j], 16)
            for j in range(GPB):
                gather(16, j)
            with pool.Fori(32, 16 * BODIES + 16, 16) as count:
                for j in range(GPB):
                    gather(count, j)

        @block.scalar
        def _(act):
            def scale_matches(i, j):
                g, q, e0 = GPB * i + j, j // 2, (j % 2) * TPG
                act.wait_ge(hid_done, g + 1)
                at_least(act, w_done, g - 1)
                nc.scalar.activation(hidden[j % 2][:, :], ps_h[0:layer.hid, 0:layer.group_cols], ACT.Silu,
                                     scale=layer.silu_scale).then_inc(silu_done, 1)
                if j % 2 == 0:
                    act.wait_ge(attr_in[q], 16 * i + 16)
                act.wait_ge(matched, g + 1)
                for t in range(TPG):
                    for c, e in enumerate((1, 2, 3, 0)[:layer.act_scales]):
                        last = nc.scalar.activation(match[j][:, t, c, :], match[j][:, t, 4, :], ACT.Copy,
                                                    scale=attr[q][:, e0 + t, e:e + 1])
                last.then_inc(scaled, 1)
            group_loop(act, scale_matches)

        @block.tensor
        def _(pe):
            def hid(i, j):
                if j % 2 == 0:
                    pe.wait_ge(inputs_in[j // 2], 16 * i + 16)
                at_least(pe, silu_done, GPB * i + j)
                n = layer.group_cols
                nc.tensor.matmul(ps_h[0:layer.hid, 0:n], w[f"fc1_{L}"][:, :], inputs[j // 2][:, (j % 2) * n:(j % 2) * n + n],
                                 start=True, stop=True).then_inc(hid_done, 1)

            def edge_weights(i, o):
                j = o % GPB
                pe.wait_ge(silu_done, GPB * i + o + 1)
                used, body = (o - 2) % GPB, i + (o - 2) // GPB
                if not (isinstance(body, int) and body < 0):
                    pe.wait_ge(msg_done[used], 16 * body + MSG0 + 16)
                for u in range(TPG // layer.tiles_per_product):
                    c0, n = u * layer.tiles_per_product * WPITCH, w[f"fc2_{L}"].shape[1]
                    last = nc.tensor.matmul(ps_w[j % 2][:, c0:c0 + n], hidden[j % 2][:, u * P:(u + 1) * P], w[f"fc2_{L}"][:, :],
                                            start=True, stop=True)
                last.then_inc(w_done, 1)

            def window_sums(j, m5):
                out, m = ps_sum[j % 2], msg[j % 2]
                for t in range(TPG):
                    def product(rows, c0, f, which, n=1, first=False, end=False):
                        return nc.tensor.matmul(out[rows, c0:c0 + n, :], m[:, t, f:f + rows.stop - rows.start],
                                                m5[:, t, which:which + n, :], start=(first and t == 0),
                                                stop=(end and t == TPG - 1))
                    product(slice(0, 64), 0, 64, 0, n=3, first=True, end=(L == 0))
                    product(slice(64, 128), 2, 0, 3, first=True)
                    product(slice(64, 128), 0, 128, 3)
                    product(slice(64, 96), 1, 192, 3, end=(L == 0))
                    for c in range(3):
                        last = product(slice(96, 128), 1, 224 + V * c, c, end=(L == 0 and c == 2))
                    if L == 1:
                        product(slice(0, 64), 3, 320, 4, end=True)
                        last = product(slice(64, 128), 3, 384, 4, end=True)
                return last

            def sum_group(i, o):
                g, j = GPB * i + o, o % GPB
                extras = pe.value_load(w["table"][0:1, bass.ds(g, 1), 1:2], min_val=0, max_val=NPAD // WIN - 1)
                pe.wait_ge(msg_done[j], 16 * (i + o // GPB) + MSG0 + 16)
                pe.wait_ge(scaled, g + 1)
                window_sums(j, match[j]).then_inc(sum_done, 1)
                with pe.If(extras):
                    before = pe.value_load(w["table"][0:1, bass.ds(g, 1), 2:3], min_val=0, max_val=G * (NPAD // WIN))
                    with pe.Fori(0, extras) as x:
                        pe.wait_ge(x_matched, before + x + 1)
                        window_sums(j, match_x).then_inc(x_sum_done, 1)

            for j in range(GPB):
                hid(0, j)
                if j >= 1:
                    edge_weights(0, j - 1)
                if j >= 2:
                    sum_group(0, j - 2)
            pe.wait_ge(silu_done, GPB)
            for c in range(WARM_UP):
                nc.tensor.matmul(ps_h[:, 0:480], w["ident"][:, :], w["out1"][:, :], start=True, stop=True)
            with pe.Fori(1, BODIES) as i:
                for j in range(GPB):
                    hid(i, j)
                    edge_weights(i, j - 1)
                    sum_group(i, j - 2)
            edge_weights(BODIES, -1)
            sum_group(BODIES, -2)
            sum_group(BODIES, -1)

        @block.vector
        def _(dve):
            if L == 0:
                for q in range(2):
                    nc.vector.memset(inputs[q][:, :], 0.0).then_inc(zeroed, 1)
            for b in range(2):
                nc.vector.memset(msg[b][:, :, 416:448], 0.0)
            nc.vector.memset(dst_rel[:, T:T + AHEAD * TPG], 0.0)
            for j in range(GPB):
                nc.vector.memset(e_kept[j % 2][:, (j // 2) * TPG:(j // 2 + 1) * TPG, :], 0.0).then_inc(msg_done[j], MSG0)
            nc.vector.tensor_copy(iota, w["iota"][:, :]).then_inc(prepared, 1)
            dve.wait_ge(prepared, 1)
            dve.wait_ge(dst_in, 16)
            iota_t = iota.unsqueeze(1).broadcast_to([P, TPG, WIN])

            def rel_of(g):
                return dst_rel[:, bass.ds(g * TPG, TPG)]

            def match_group(g, into):
                return nc.vector.tensor_tensor(into[:, :, 4, :], iota_t, rel_of(g).unsqueeze(2).broadcast_to([P, TPG, WIN]),
                                               ALU.is_equal)

            def window_of(g):
                both = dve.value_load(w["table"][0:1, bass.ds(g, 1), 0:1], min_val=0, max_val=(NPAD << EXTRA_BITS) - 1)
                return (nc.s_assert_within(both >> EXTRA_BITS, 0, NPAD - 1,
                                           skip_runtime_bounds_check_because="setup keeps destinations below NPAD"),
                        nc.s_assert_within(both & ((1 << EXTRA_BITS) - 1), 0, NPAD // WIN - 1,
                                           skip_runtime_bounds_check_because="a span is below NPAD"))

            def add_group(i, o, window_at, earlier, count):
                g, j = GPB * i + o, o % GPB
                start, extras = window_at
                window = ps_sum[j % 2][:, 0:layer.chunks, :]
                dve.wait_ge(sum_done, g + 1)
                dve.wait_ge(earlier, count)
                at = sums[:, 0:layer.chunks, bass.ds(start, WIN)]
                nc.vector.tensor_tensor(at, at, window, ALU.add).then_inc(added, 1)
                with dve.If(extras):
                    before = dve.value_load(w["table"][0:1, bass.ds(g, 1), 2:3], min_val=0, max_val=G * (NPAD // WIN))
                    with dve.Fori(0, extras) as x:
                        dve.wait_ge(added, g + 1)
                        nc.vector.tensor_scalar(rel_of(g), rel_of(g), -float(WIN), None, ALU.add).then_inc(x_rel, 1)
                        dve.wait_ge(x_rel, 2 * (before + x) + 1)
                        match_group(g, match_x).then_inc(x_rel, 1)
                        dve.wait_ge(x_rel, 2 * (before + x) + 2)
                        for c, e in enumerate((1, 2, 3, 0)):
                            e0 = (j % 2) * TPG
                            last = nc.vector.tensor_tensor(
                                match_x[:, :, c, :], match_x[:, :, 4, :],
                                e_kept[j // 2][:, e0:e0 + TPG, e:e + 1].broadcast_to([P, TPG, WIN]), ALU.mult)
                        last.then_inc(x_matched, 1)
                        dve.wait_ge(x_sum_done, before + x + 1)
                        there = nc.s_assert_within(
                            start + (x + 1) * WIN, 0, NPAD - 1,
                            skip_runtime_bounds_check_because="extras count the whole windows up to a destination below NPAD")
                        at = sums[:, 0:layer.chunks, bass.ds(there, WIN)]
                        nc.vector.tensor_tensor(at, at, window, ALU.add).then_inc(x_added, 1)
                        dve.wait_ge(x_added, before + x + 1)

            def messages(i, j):
                g, q, e0 = GPB * i + j, j // 2, (j % 2) * TPG
                if j % 2 == 0:
                    dve.wait_ge(attr_in[q], 16 * i + 16)
                    if not (isinstance(i, int) and g == 0):
                        dve.wait_ge(msg_done[(j - 1) % GPB], 16 * (i + (j - 1) // GPB) + MSG0 + 16)
                    nc.vector.tensor_copy(e_p, attr[q][:, :, :])
                    nc.vector.tensor_copy(e_kept[q][:, :, :], attr[q][:, :, :]).then_inc(e_copied, 1)
                match_group(g + AHEAD, match[(j + AHEAD) % GPB]).then_inc(matched, 1)
                if j % 2 == 0:
                    dve.wait_ge(e_copied, 2 * i + q + 1)
                r, m = rows[j], msg[j % 2]

                def comps(ap):
                    return ap.rearrange("p t (c n) -> p t c n", n=V)

                if layer.act_scales == 3:
                    dve.wait_ge(matched, g + 1)
                    nc.vector.tensor_tensor(match[j][:, :, 3, :], e_p[:, e0:e0 + TPG, 0:1].broadcast_to([P, TPG, WIN]),
                                            match[j][:, :, 4, :], ALU.mult)
                if L == 1:
                    dve.wait_ge(gathered[j], GATHERED * i + GATHERED)

                    def e3(c):
                        return e_p[:, e0:e0 + TPG, c:c + 3].unsqueeze(3).broadcast_to([P, TPG, 3, V])
                    nc.vector.tensor_tensor(comps(cross_a), e3(3), comps(r[:, :, 96:192]), ALU.mult)
                    nc.vector.tensor_tensor(comps(cross_b[:, :, :]), e3(2), comps(r[:, :, 128:224]), ALU.mult).then_inc(crossed, 1)
                if L == 0:
                    dve.wait_ge(gathered[j], GATHERED * i + GATHERED)
                dve.wait_ge(w_done, g + 1)
                wt = ps_w[j % 2][:, :].rearrange("p (t n) -> p t n", n=WPITCH)

                def w_v(w0):
                    return wt[:, :, w0:w0 + V].unsqueeze(2).broadcast_to([P, TPG, 3, V])

                nc.vector.tensor_tensor(m[:, :, 0:128].rearrange("p t (k n) -> p t k n", k=2),
                                        wt[:, :, 0:128].rearrange("p t (k n) -> p t k n", k=2),
                                        r[:, :, 0:S].unsqueeze(2).broadcast_to([P, TPG, 2, S]), ALU.mult)
                if L == 1:
                    dve.wait_ge(crossed, g + 1)
                    nc.vector.tensor_tensor(m[:, :, 320:416], cross_a, cross_b[:, :, :], ALU.subtract).then_inc(subtracted, 1)
                nc.vector.tensor_tensor(comps(m[:, :, 128:224]), w_v(128), comps(r[:, :, 64:160]), ALU.mult)
                window_at = None if isinstance(g, int) and g == 0 else window_of(g - 1)
                last = nc.vector.tensor_tensor(comps(m[:, :, 224:320]), w_v(160), comps(r[:, :, 64:160]), ALU.mult)
                if L == 1:
                    dve.wait_ge(subtracted, g + 1)
                    last = nc.vector.tensor_tensor(comps(m[:, :, 320:416]), w_v(192), comps(m[:, :, 320:416]), ALU.mult)
                last.then_inc(msg_done[j], 16)
                return window_at

            for g in range(AHEAD):
                match_group(g, match[g]).then_inc(matched, 1)
            for j in range(GPB):
                window_at = messages(0, j)
                if j >= 1:
                    add_group(0, j - 1, window_at, matched, j + 1 + AHEAD)
            with dve.Fori(1, BODIES) as i:
                for j in range(GPB):
                    window_at = messages(i, j)
                    add_group(i, j - 1, window_at, matched, GPB * i + j + 1 + AHEAD)
            add_group(BODIES, -1, window_of(G - 1), added, G - 1)
            dve.wait_ge(added, G)


def layer0_nodes_phase(nc, d, w, sums):
    with ExitStack() as ctx:
        def sb(name, shape):
            return ctx.enter_context(nc.sbuf_tensor(f"m_{name}", shape, F32))

        def psum(name, shape):
            return ctx.enter_context(nc.psum_tensor(f"m_{name}", shape, F32))

        def sem(name):
            return ctx.enter_context(nc.semaphore(f"m_{name}"))

        R1 = D + V3 + S1
        x_v = [sb(f"xv{s}", [V3, TPU * P]) for s in range(UPB)]
        x_s = [sb(f"xs{s}", [S, TPU * P]) for s in range(UPB)]
        x_row = [sb(f"xrow{s}", [P, TPU, D]) for s in range(UPB)]
        x1 = [sb(f"x1_{s}", [P, TPU, D]) for s in range(UPB)]
        h1 = [sb(f"h1_{s}", [P, TPU, R1]) for s in range(UPB)]
        staged = [sb(f"staged{b}", [P, 3, P]) for b in range(2)]
        y = [[sb(f"y{b}_{c}", [P, D]) for c in range(4)] for b in range(2)]
        stats = [sb(f"stats{b}", [P, 6]) for b in range(2)]
        moments = [sb(f"moments{b}", [P, 2]) for b in range(2)]
        var = [sb(f"var{b}", [P, 1]) for b in range(2)]
        dev = [sb(f"dev{b}", [P, 1]) for b in range(2)]
        inv_dev = [sb(f"inv_dev{b}", [P, 1]) for b in range(2)]
        x1T_v = [sb(f"x1Tv{b}", [V3, P]) for b in range(2)]
        x1T_s = [sb(f"x1Ts{b}", [S, P]) for b in range(2)]
        ps_self = [psum(f"self{b}", [P, 512]) for b in range(2)]
        ps_agg = [psum(f"agg{b}", [P, 512]) for b in range(2)]
        ps_tr = [psum(f"tr{b}", [P, 512]) for b in range(2)]
        ps_next = [psum(f"next{b}", [P, 512]) for b in range(2)]

        loaded = [sem(f"loaded{s}") for s in range(UPB)]
        stored = [sem(f"stored{s}") for s in range(UPB)]
        stage_done, out_mm, chain, y_ready, statted, momented, var_ready = (
            sem(n) for n in ("stage_done", "out_mm", "chain", "y_ready", "statted", "momented", "var_ready"))
        dev_ready, inv_ready, x1_ready, tr_done, trs_copied, next_mm, h1_ready = (
            sem(n) for n in ("dev_ready", "inv_ready", "x1_ready", "tr_done", "trs_copied", "next_mm", "h1_ready"))
        block = ctx.enter_context(nc.Block())

        def pipeline(engine, stages):
            per = TPU * UPB

            def turn(i, j):
                for lag, step in stages:
                    if isinstance(i, int) and not 0 <= per * i + j - lag < NT:
                        continue
                    o = j - lag
                    body = i + o // per
                    step(per * i + o, body, (o % per) // TPU, o % TPU, o % 2)
            for j in range(per):
                turn(0, j)
            with engine.Fori(1, NBODY) as i:
                for j in range(per):
                    turn(i, j)
            for j in range(max(lag for lag, _ in stages)):
                turn(NBODY, j)

        @block.gpsimd
        def _(pool):
            def load(unit, i, s):
                at_least(pool, y_ready, TPU * unit - TPU)
                cols = bass.ds(unit * (TPU * P), TPU * P)
                pool.dma_start(x_v[s][:, :], d["xT_v"][:, cols]).then_inc(loaded[s], 16)
                pool.dma_start(x_s[s][:, :], d["xT_s"][:, cols]).then_inc(loaded[s], 16)
                pool.dma_start(x_row[s][:, :, :], d["x"][cols, :].rearrange("(k p) n -> p k n", p=P)).then_inc(loaded[s], 16)
            unit_loop(pool, load)
            pool.wait_ge(stage_done, NT)
            nc.gpsimd.memset(sums[:, 0:3, :], 0.0)

        @block.sync
        def _(sp):
            def store(unit, i, s):
                nodes = bass.ds(unit * (TPU * P), TPU * P)

                def rows(name):
                    return d[name][nodes, :].rearrange("(k p) n -> p k n", p=P)
                sp.wait_ge(x1_ready, TPU * unit + TPU)
                sp.dma_start(rows("x1"), x1[s][:, :, :]).then_inc(stored[s], 16)
                sp.wait_ge(h1_ready, TPU * unit + TPU)
                sp.dma_start(rows("table1")[:, :, 0:S], h1[s][:, :, V3:D]).then_inc(stored[s], 16)
                sp.dma_start(rows("table1")[:, :, S:D], h1[s][:, :, 0:V3]).then_inc(stored[s], 16)
                sp.dma_start(rows("table1")[:, :, D:D + 2 * V], h1[s][:, :, 0:2 * V]).then_inc(stored[s], 16)
                sp.dma_start(rows("self1"), h1[s][:, :, D:R1]).then_inc(stored[s], 16)
            unit_loop(sp, store)
            for s in range(UPB):
                sp.wait_ge(stored[s], 80 * NBODY)

        @block.scalar
        def _(act):
            def stage(n, i, s, k, b):
                at_least(act, out_mm, n - 1)
                nc.scalar.activation(staged[b][:, :, :], sums[:, 0:3, bass.ds(n * P, P)], ACT.Copy).then_inc(stage_done, 1)

            def deviation(n, i, s, k, b):
                act.wait_ge(var_ready, n + 1)
                at_least(act, inv_ready, n - 1)
                nc.scalar.activation(dev[b][:, :], var[b][:, :], ACT.Sqrt).then_inc(dev_ready, 1)

            def copy_transposed(n, i, s, k, b):
                act.wait_ge(tr_done, n + 1)
                at_least(act, next_mm, n - 1)
                nc.scalar.activation(x1T_v[b][:, :], ps_tr[b][0:V3, 0:P], ACT.Copy)
                nc.scalar.activation(x1T_s[b][:, :], ps_tr[b][0:S, P:2 * P], ACT.Copy).then_inc(trs_copied, 1)

            def scale_next(n, i, s, k, b):
                act.wait_ge(next_mm, n + 1)
                nc.scalar.activation(h1[s][:, k, :], ps_next[b][:, 0:R1], ACT.Copy,
                                     scale=w["attr"][:, bass.ds(n, 1), 0]).then_inc(h1_ready, 1)
            pipeline(act, ((0, stage), (3, deviation), (6, copy_transposed), (8, scale_next)))

        @block.tensor
        def _(pe):
            def output(n, i, s, k, b):
                if k == 0:
                    pe.wait_ge(loaded[s], 48 * i + 48)
                pe.wait_ge(stage_done, n + 1)
                at_least(pe, y_ready, n - 1)
                mine = ps_self[b][:, 0:2 * D].rearrange("p (a n) -> p a n", a=2)
                nc.tensor.matmul(mine[:, :, 0:V3], x_v[s][:, k * P:(k + 1) * P], w["node_v0"][:, 192:384], start=True, stop=True)
                nc.tensor.matmul(mine[:, :, V3:D], x_s[s][:, k * P:(k + 1) * P], w["node_s0"][:, 128:256], start=True, stop=True)
                agg = ps_agg[b][:, 0:2 * D].rearrange("p (a n) -> p a n", a=2)
                nc.tensor.matmul(agg, staged[b][:, 1, :], w["out0"][:, 0:320], start=True, stop=False)
                nc.tensor.matmul(agg[:, :, 0:64], staged[b][:, 0, :], w["out0"][:, 320:448], start=False, stop=False)
                nc.tensor.matmul(agg[:, :, 64:160], staged[b][:, 2, :], w["out0"][:, 448:640], start=False,
                                 stop=True).then_inc(out_mm, 1)

            def transpose(n, i, s, k, b):
                pe.wait_ge(x1_ready, n + 1)
                at_least(pe, trs_copied, n - 1)
                nc.tensor.transpose(ps_tr[b][0:V3, 0:P], x1[s][:, k, 0:V3], w["ident"][:, :])
                nc.tensor.transpose(ps_tr[b][0:S, P:2 * P], x1[s][:, k, V3:D], w["ident"][:, :]).then_inc(tr_done, 1)

            def next_layer(n, i, s, k, b):
                pe.wait_ge(trs_copied, n + 1)
                at_least(pe, h1_ready, n - 1)
                both = ps_next[b][:, 0:2 * D].rearrange("p (a n) -> p a n", a=2)
                nc.tensor.matmul(both[:, :, 0:V3], x1T_v[b][:, :], w["node_v1"][:, :], start=True, stop=True)
                nc.tensor.matmul(ps_next[b][:, V3:D], x1T_s[b][:, :], w["node_s1"][:, 0:64], start=True, stop=True)
                nc.tensor.matmul(ps_next[b][:, D + V3:R1], x1T_s[b][:, :], w["node_s1"][:, 64:160], start=True,
                                 stop=True).then_inc(next_mm, 1)
            pipeline(pe, ((1, output), (5, transpose), (7, next_layer)))

        @block.vector
        def _(dve):
            def residual(n, i, s, k, b):
                dve.wait_ge(out_mm, n + 1)
                if k == 0:
                    dve.wait_ge(loaded[s], 48 * i + 48)
                a, c = (w["attr"][:, bass.ds(n, 1), x] for x in range(2))
                am, cm = (w["masked"][:, bass.ds(n, 1), x] for x in range(2))
                terms = ((ps_self, 0, a), (ps_self, D, c), (ps_agg, 0, am), (ps_agg, D, cm))
                before = x_row[s][:, k, :]
                for x, (bank, c0, factor) in enumerate(terms):
                    if x:
                        dve.wait_ge(chain, 3 * n + x)
                    step = nc.vector.scalar_tensor_tensor(out=y[b][x][:, :], in0=bank[b][:, c0:c0 + D], scalar=factor,
                                                          in1=before, op0=ALU.mult, op1=ALU.add)
                    before = y[b][x][:, :]
                    step.then_inc(chain if x < 3 else y_ready, 1)
                dve.wait_ge(y_ready, n + 1)
                nc.vector.bn_stats(stats[b][:, :], y[b][3][:, :]).then_inc(statted, 1)
                dve.wait_ge(out_mm, 1)
                dve.wait_ge(statted, n + 1)
                nc.vector.bn_aggr(moments[b][:, :], stats[b][:, :]).then_inc(momented, 1)
                dve.wait_ge(momented, n + 1)
                at_least(dve, dev_ready, n - 1)
                nc.vector.tensor_scalar(var[b][:, :], moments[b][:, 1:2], EPS, None, ALU.add).then_inc(var_ready, 1)

            def normalize(n, i, s, k, b):
                dve.wait_ge(dev_ready, n + 1)
                nc.vector.reciprocal(inv_dev[b][:, :], dev[b][:, :]).then_inc(inv_ready, 1)
                dve.wait_ge(inv_ready, n + 1)
                if k == 0:
                    at_least(dve, stored[s], 80 * i)
                nc.vector.tensor_scalar(x1[s][:, k, :], y[b][3][:, :], moments[b][:, 0:1], inv_dev[b][:, :],
                                        ALU.subtract, ALU.mult).then_inc(x1_ready, 1)
            pipeline(dve, ((4, normalize), (2, residual)))


def layer1_nodes_phase(nc, d, w, sums):
    with ExitStack() as ctx:
        def sb(name, shape):
            return ctx.enter_context(nc.sbuf_tensor(f"f_{name}", shape, F32))

        def sem(name):
            return ctx.enter_context(nc.semaphore(f"f_{name}"))

        O1 = V3 + S1
        x_row = [sb(f"xrow{s}", [P, TPU, D]) for s in range(UPB)]
        self_row = [sb(f"self{s}", [P, TPU, O1]) for s in range(UPB)]
        staged = [sb(f"staged{b}", [P, 4, P]) for b in range(2)]
        pre = [sb(f"pre{b}", [P, O1]) for b in range(2)]
        silu = [sb(f"silu{b}", [P, S]) for b in range(2)]
        tanh = [sb(f"tanh{b}", [P, V]) for b in range(2)]
        gate = [sb(f"gate{b}", [P, V]) for b in range(2)]
        gated = [sb(f"gated{b}", [P, V3]) for b in range(2)]
        y = [sb(f"y{b}", [P, D]) for b in range(2)]
        centred = sb("centred", [P, NT, D])
        stats = [sb(f"stats{b}", [P, 6]) for b in range(2)]
        moments = [sb(f"moments{b}", [P, 2]) for b in range(2)]
        var, dev, inv_dev = sb("var", [P, NT]), sb("dev", [P, NT]), sb("inv_dev", [P, NT])
        ps = [ctx.enter_context(nc.psum_tensor(f"f_ps{b}", [P, 512], F32)) for b in range(2)]

        loaded = [sem(f"loaded{s}") for s in range(UPB)]
        stage_done, out_mm, pre_ready, acted, chain, y_ready, statted, momented = (
            sem(n) for n in ("stage_done", "out_mm", "pre_ready", "acted", "chain", "y_ready", "statted", "momented"))
        var_ready, dev_ready, inv_ready, normed, stored = (
            sem(n) for n in ("var_ready", "dev_ready", "inv_ready", "normed", "stored"))
        block = ctx.enter_context(nc.Block())

        @block.gpsimd
        def _(pool):
            def load(unit, i, s):
                at_least(pool, y_ready, TPU * unit - TPU)
                nodes = bass.ds(unit * (TPU * P), TPU * P)
                pool.dma_start(x_row[s][:, :, :], d["x1"][nodes, :].rearrange("(k p) n -> p k n", p=P)).then_inc(loaded[s], 16)
                pool.dma_start(self_row[s][:, :, :], d["self1"][nodes, :].rearrange("(k p) n -> p k n", p=P)
                               ).then_inc(loaded[s], 16)
            unit_loop(pool, load)

        @block.scalar
        def _(act):
            def stage(n, b):
                at_least(act, out_mm, n - 1)
                nc.scalar.activation(staged[b][:, :, :], sums[:, :, bass.ds(n * P, P)], ACT.Copy).then_inc(stage_done, 1)

            def gates(n, b):
                act.wait_ge(pre_ready, n + 1)
                at_least(act, y_ready, n - 1)
                nc.scalar.activation(silu[b][:, :], pre[b][:, V3:V3 + S], ACT.Silu)
                nc.scalar.activation(tanh[b][:, :], pre[b][:, V3 + S:O1], ACT.Tanh, scale=0.5).then_inc(acted, 1)

            stage(0, 0)

            def turn(n, unit, i, s, k):
                b = (TPU * s + k) % 2
                stage(n + 1, 1 - b)
                gates(n, b)
            for j in range(TPU * UPB):
                turn(j, 0, 0, j // TPU, j % TPU)
            with act.Fori(1, NBODY - 1) as i:
                for j in range(TPU * UPB):
                    turn(TPU * UPB * i + j, 0, i, j // TPU, j % TPU)
            for n in range(NT - TPU * UPB, NT):
                if n + 1 < NT:
                    stage(n + 1, (n + 1) % 2)
                gates(n, n % 2)
            act.wait_ge(var_ready, NT)
            nc.scalar.activation(dev[:, :], var[:, :], ACT.Sqrt).then_inc(dev_ready, 1)

        @block.tensor
        def _(pe):
            def output(n, unit, i, s, k):
                b = (TPU * s + k) % 2
                pe.wait_ge(stage_done, n + 1)
                at_least(pe, pre_ready, n - 1)
                o = ps[b]
                nc.tensor.matmul(o[:, 0:O1], staged[b][:, 1, :], w["out1"][:, 0:192], start=True, stop=False)
                nc.tensor.matmul(o[:, 0:64], staged[b][:, 0, :], w["out1"][:, 192:256], start=False, stop=False)
                nc.tensor.matmul(o[:, 64:O1], staged[b][:, 2, :], w["out1"][:, 256:384], start=False, stop=False)
                nc.tensor.matmul(o[:, 0:V3], staged[b][:, 3, :], w["out1"][:, 384:480], start=False, stop=True).then_inc(out_mm, 1)
            node_loop(pe, output)

        @block.vector
        def _(dve):
            def before_gates(n, i, s, k, b):
                dve.wait_ge(out_mm, n + 1)
                if k == 0:
                    dve.wait_ge(loaded[s], 32 * i + 32)
                at_least(dve, acted, n - 1)
                nc.vector.scalar_tensor_tensor(out=pre[b][:, :], in0=ps[b][:, 0:O1], scalar=w["attr"][:, bass.ds(n, 1), 0],
                                               in1=self_row[s][:, k, :], op0=ALU.mult, op1=ALU.add).then_inc(pre_ready, 1)

            def after_gates(n, i, s, k, b):
                dve.wait_ge(acted, n + 1)
                nc.vector.tensor_scalar(gate[b][:, :], tanh[b][:, :], 1.0, 0.5, ALU.add, ALU.mult).then_inc(chain, 1)
                nc.vector.tensor_tensor(y[b][:, V3:D], silu[b][:, :], x_row[s][:, k, V3:D], ALU.add)
                dve.wait_ge(chain, 2 * n + 1)
                nc.vector.tensor_tensor(gated[b][:, :].rearrange("p (c n) -> p c n", n=V),
                                        pre[b][:, 0:V3].rearrange("p (c n) -> p c n", n=V),
                                        gate[b][:, :].unsqueeze(1).broadcast_to([P, 3, V]), ALU.mult).then_inc(chain, 1)
                dve.wait_ge(chain, 2 * n + 2)
                nc.vector.tensor_tensor(y[b][:, 0:V3], gated[b][:, :], x_row[s][:, k, 0:V3], ALU.add).then_inc(y_ready, 1)
                dve.wait_ge(y_ready, n + 1)
                nc.vector.bn_stats(stats[b][:, :], y[b][:, :]).then_inc(statted, 1)
                dve.wait_ge(out_mm, 1)
                dve.wait_ge(statted, n + 1)
                nc.vector.bn_aggr(moments[b][:, :], stats[b][:, :]).then_inc(momented, 1)
                dve.wait_ge(momented, n + 1)
                nc.vector.tensor_scalar(centred[:, bass.ds(n, 1), :], y[b][:, :].unsqueeze(1), moments[b][:, 0:1], None, ALU.subtract)
                nc.vector.tensor_scalar(var[:, bass.ds(n, 1)], moments[b][:, 1:2], EPS, None, ALU.add).then_inc(var_ready, 1)

            before_gates(0, 0, 0, 0, 0)
            per = TPU * UPB

            def turn(i, j):
                o = j + 1
                before_gates(per * i + o, i + o // per, (o % per) // TPU, o % TPU, o % 2)
                after_gates(per * i + j, i, j // TPU, j % TPU, j % 2)
            for j in range(per):
                turn(0, j)
            with dve.Fori(1, NBODY - 1) as i:
                for j in range(per):
                    turn(i, j)
            for j in range(per - 1):
                turn(NBODY - 1, j)
            after_gates(NT - 1, NBODY - 1, UPB - 1, TPU - 1, (NT - 1) % 2)

            dve.wait_ge(dev_ready, 1)
            nc.vector.reciprocal(inv_dev[:, :], dev[:, :]).then_inc(inv_ready, 1)
            dve.wait_ge(inv_ready, 1)
            with dve.Fori(0, NBODY) as u:
                for k in range(TPU * UPB):
                    n = u * (TPU * UPB) + k
                    row = centred[:, bass.ds(n, 1), :]
                    nc.vector.tensor_scalar(row, row, inv_dev[:, bass.ds(n, 1)], None, ALU.mult).then_inc(normed, 1)

        @block.sync
        def _(sp):
            with sp.Fori(0, NT // TPU) as u:
                sp.wait_ge(normed, TPU * u + TPU)
                sp.dma_start(d["out"][bass.ds(u * (TPU * P), TPU * P), :].rearrange("(k p) n -> p k n", p=P),
                             centred[:, bass.ds(u * TPU, TPU), :]).then_inc(stored, 16)
            sp.wait_ge(stored, 16 * (NT // TPU))


INPUTS = (
    ("x", (NPAD, D), F32), ("xT_v", (V3, NPAD), F32), ("xT_s", (S, NPAD), F32), ("attr", (P, NT, 3), F32),
    ("src", (P, T), I32), ("dst_tile", (P, T), I32), ("dst_by_group", (GP, GQ, GE), I32),
    ("edge_attr", (P, T, 6), F32), ("inputs0", (NB0, EPAD), F32), ("inputs1", (2 * NB1, EPAD // 2), F32),
    ("fc1_0", (P, H0), F32), ("fc2_0", (H0, 192), F32), ("fc1_1", (P, P), F32), ("fc2_1", (P, 480), F32),
    ("node_s0", (S, 256), F32), ("node_v0", (V3, 384), F32), ("node_s1", (S, 160), F32), ("node_v1", (V3, 192), F32),
    ("out1", (P, 480), F32), ("l2", (MID, 16, P), F32), ("l3", (MID, S + V), F32),
)
SCRATCH = (
    ("table0", (NPAD, D), F32), ("table1", (NPAD, D + 2 * V), F32), ("x1", (NPAD, D), F32), ("self1", (NPAD, V3 + S1), F32),
    ("lo_dram", (G,), I32), ("extra_dram", (G,), I32), ("dst_rel", (P, T), F32),
)


def build(nc):
    d = {name: nc.dram_tensor("in_" + name, shape, dt, kind="ExternalInput").ap() for name, shape, dt in INPUTS}
    d["out"] = nc.dram_tensor("out", (NPAD, D), F32, kind="ExternalOutput").ap()
    for name, shape, dt in SCRATCH:
        d[name] = nc.dram_tensor("scratch_" + name, shape, dt).ap()
    with ExitStack() as ctx:
        w = kept_tensors(nc, ctx)
        sums = ctx.enter_context(nc.sbuf_tensor("sums", [P, 4, SUMW], F32))
        setup_phase(nc, d, w, sums)
        edge_phase(nc, d, w, sums, Layer(0))
        layer0_nodes_phase(nc, d, w, sums)
        edge_phase(nc, d, w, sums, Layer(1))
        layer1_nodes_phase(nc, d, w, sums)


def lay_out(inputs):
    a = {k: np.asarray(v) for k, v in inputs.items()}
    f = np.float32

    def padded(v, n, fill=0):
        out = np.full((n,) + v.shape[1:], fill, v.dtype)
        out[:v.shape[0]] = v
        return out

    def by_partition(v):
        return np.ascontiguousarray(np.swapaxes(v.reshape((-1, P) + v.shape[1:]), 0, 1))

    def diagonal(*blocks):
        out = np.zeros((V3, V3 * len(blocks)), f)
        for k, block in enumerate(blocks):
            for c in range(3):
                out[V * c:V * c + V, V3 * k + V * c:V3 * k + V * c + V] = block
        return out

    x = padded(a["x"], NPAD)
    xv = x[:, S:].reshape(NPAD, V, 3).transpose(0, 2, 1).reshape(NPAD, V3)
    r = {"x": np.concatenate([xv, x[:, :S]], 1), "xT_v": xv.T.copy(), "xT_s": x[:, :S].T.copy()}
    r["attr"] = by_partition(padded(np.concatenate([a["node_vec1"], a["node_vec1_n2"], a["node_vec1_n3"]], 1), NPAD))
    r["src"] = by_partition(padded(a["src"], EPAD))
    dst = padded(a["dst"], EPAD, NODES)
    r["dst_tile"] = by_partition(dst)
    r["dst_by_group"] = dst.reshape(GP, GQ, GE)
    e = padded(a["edge_attr_4"], EPAD)
    r["edge_attr"] = by_partition(np.concatenate([e, e[:, 1:3]], 1))
    r["inputs0"] = padded(a["edge_attr_10"], EPAD).T.copy()
    r["inputs1"] = padded(a["edge_attr_64"], EPAD).reshape(T // 2, 2, P, NB1).transpose(1, 3, 0, 2).reshape(2 * NB1, EPAD // 2)
    L0 = {k[7:]: v for k, v in a.items() if k.startswith("L0_gnn_")}
    L1 = {k[7:]: v for k, v in a.items() if k.startswith("L1_gnn_")}
    r["fc1_0"], r["fc2_0"] = padded(L0["W_fc1"], P), L0["W_fc2"]
    r["fc1_1"] = np.zeros((P, P), f)
    r["fc1_1"][:H1, :H1] = r["fc1_1"][H1:, H1:] = L1["fc_w1"]
    r["fc2_1"] = np.zeros((P, 480), f)
    r["fc2_1"][:H1, :224] = r["fc2_1"][H1:, WPITCH:] = L1["fc_w2"]
    names = ("l1_a", "l1_c", "sc_a", "sc_c")
    r["node_s0"] = np.concatenate([L0["Ws_" + n] for n in names], 1)
    r["node_v0"] = diagonal(*(L0["Wv_" + n] for n in names))
    r["node_s1"] = np.concatenate([L1["lin1_ws"], L1["sc_ws"]], 1)
    r["node_v1"] = diagonal(L1["lin1_wv"], L1["sc_wv"])
    v, s, o = L1["lin2_wv"], L1["lin2_ws"], np.zeros((P, 480), f)
    o[0:64, 32:64] = o[0:64, 192:224] = o[0:64, 256:288] = v[0:64]
    o[64:96, 64:96] = o[64:96, 192:224] = o[96:128, 224:256] = v[64:96]
    o[96:128, 96:192], o[64:128, 288:384] = s[64:96], s[0:64]
    for c in range(3):
        o[V * c:V * c + V, 384 + V * c:384 + V * c + V] = v[96:128]
    r["out1"] = o
    l2 = np.zeros((MID, 16, P), f)
    for k, attr in enumerate("ac"):
        sT, vT = L0["Ws_l2_" + attr].T, L0["Wv_l2_" + attr].T
        for block in (3 * k + 1, 8 + 2 * k, 12 + k):
            l2[:, block, 0:64] = vT[:, 0:64]
        l2[:, 8 + 2 * k, 64:96] = l2[:, 9 + 2 * k, 96:128] = l2[:, 3 * k + 2, 64:96] = vT[:, 64:96]
        l2[:, 6 + k, 96:128], l2[:, 14 + k, 64:128] = sT[:, 64:96], sT[:, 0:64]
    r["l2"] = l2
    r["l3"] = np.concatenate([L0["Ws_l3"], L0["Wv_l3"]], 1)
    return {"in_" + k: np.ascontiguousarray(v) for k, v in r.items()}


def kernel(**inputs):
    import concourse.bacc as bacc
    from concourse.bass_utils import run_bass_kernel_spmd

    nc = bacc.Bacc("TRN2", target_bir_lowering=False, num_devices=1)
    build(nc)
    out = run_bass_kernel_spmd(nc, [lay_out(inputs)], core_ids=[0]).results[0]["out"][:NODES]
    vectors = out[:, :V3].reshape(NODES, 3, V).transpose(0, 2, 1).reshape(NODES, V3)
    return np.concatenate([out[:, V3:], vectors], 1)
```
